# Optimizing a Trainium2 kernel written in Bass

```python
import numpy as np
import jax
import jax.numpy as jnp

def _softmax(x, axis=-1):
    return jax.nn.softmax(x, axis=axis)
def _gelu(x):
    return jax.nn.gelu(x, approximate=True)
def _silu(x):
    return jax.nn.silu(x)
def _sigmoid(x):
    return jax.nn.sigmoid(x)
def _layernorm(x, axis=-1, eps=1e-5):
    m = jnp.mean(x, axis=axis, keepdims=True)
    v = jnp.var(x, axis=axis, keepdims=True)
    return (x - m) / jnp.sqrt(v + eps)
def _scatter_add(tgt, idx, src, axis=0):
    return tgt.at[idx].add(src)
def _segment_sum(src, seg, n):
    return jax.ops.segment_sum(src, seg, n)

kernel_name = 'mk_adj_resnorm_d1_adj_256_2a7fae'

def setup_inputs(seed: int = 0):
    np.random.seed(seed)
    _w = jnp.asarray
    def _rec_inputs():
        import jax
        import jax.numpy as jnp
        _gk = jax.random.key(seed)
        x = -0.0005207 + 1.001 * jax.random.normal(jax.random.fold_in(_gk, 1), (8, 2048, 256), jnp.float32)
        _w = (1.0 + jnp.arange(2048, dtype=jnp.float32)) ** -0.5
        _w = _w / _w.mean()
        _pij = jnp.clip(0.0078125 * _w[:, None] * _w[None, :], 0.0, 1.0)
        _a = jax.random.uniform(jax.random.fold_in(_gk, 2), (8, 2048, 2048)) < _pij
        adj = _a.astype(jnp.int32)
        return x, adj
    x, adj = _rec_inputs()
    def _L0_gnn_setup():
        import jax, jax.numpy as jnp
        import numpy as np
        B, N, D = (8, 1024, 256)
        H, HO = (4, 64)
        T = 5
        NEG = -1000000000.0
        EPS = 1e-06
        key = jax.random.key(seed)
        ks = jax.random.split(key, 6)
        nodes_embed = jax.random.normal(ks[0], (B, N, D), dtype=jnp.float32)
        node_adj = jax.random.randint(ks[1], (B, N, N), 0, T + 1)
        W = jax.random.normal(ks[2], (H, D, HO), dtype=jnp.float32) * (1.0 / np.sqrt(D))
        a_src = jax.random.normal(ks[3], (H, T, HO), dtype=jnp.float32) * 0.1
        a_dst = jax.random.normal(ks[4], (H, T, HO), dtype=jnp.float32) * 0.1
        bias = jnp.zeros((H, HO), dtype=jnp.float32)
        ln_gamma = jnp.ones((H, HO), dtype=jnp.float32)
        ln_beta = jnp.zeros((H, HO), dtype=jnp.float32)
        return {'nodes_embed': nodes_embed, 'node_adj': node_adj, 'W': W, 'a_src': a_src, 'a_dst': a_dst, 'bias': bias, 'ln_gamma': ln_gamma, 'ln_beta': ln_beta}
    _L0_gnn_all = _L0_gnn_setup()
    _L0_gnn_in = {k: v for k, v in _L0_gnn_all.items() if k in ('W', 'a_src', 'a_dst', 'bias', 'ln_gamma', 'ln_beta', )}
    del _L0_gnn_all

    return {
        "x": x,
        "adj": adj,
        "L0_gnn_W": _L0_gnn_in["W"],
        "L0_gnn_a_src": _L0_gnn_in["a_src"],
        "L0_gnn_a_dst": _L0_gnn_in["a_dst"],
        "L0_gnn_bias": _L0_gnn_in["bias"],
        "L0_gnn_ln_gamma": _L0_gnn_in["ln_gamma"],
        "L0_gnn_ln_beta": _L0_gnn_in["ln_beta"],
    }

def reference(x, adj, L0_gnn_W, L0_gnn_a_src, L0_gnn_a_dst, L0_gnn_bias, L0_gnn_ln_gamma, L0_gnn_ln_beta):
    import jax
    import jax.numpy as jnp
    def _L0_gnn_ref(nodes_embed, node_adj, W, a_src, a_dst, bias, ln_gamma, ln_beta):
        import jax, jax.numpy as jnp
        import numpy as np
        B, N, D = (8, 1024, 256)
        H, HO = (4, 64)
        T = 5
        NEG = -1000000000.0
        EPS = 1e-06
        h = jnp.einsum('bnd,hde->bhne', nodes_embed, W)
        e_src = jnp.einsum('bhne,hte->bhtn', h, a_src)
        e_dst = jnp.einsum('bhne,hte->bhtn', h, a_dst)
        n_types = a_src.shape[1]
        weight = jnp.zeros(h.shape[:2] + (h.shape[2], h.shape[2]), dtype=h.dtype)
        for t in range(n_types):
            mask = (node_adj == t + 1).astype(h.dtype)[:, None]
            weight = weight + mask * (e_src[:, :, t, :, None] + e_dst[:, :, t, None, :])
        weight = jax.nn.leaky_relu(weight, negative_slope=0.01)
        weight = jnp.where(node_adj[:, None] == 0, NEG, weight)
        attention = jax.nn.softmax(weight, axis=-1)
        dst = jnp.einsum('bhij,bhje->bhie', attention, h) + bias[None, :, None, :]
        out = jax.nn.relu(dst) + h
        mu = out.mean(axis=-1, keepdims=True)
        var = out.var(axis=-1, keepdims=True)
        out = (out - mu) / jnp.sqrt(var + EPS) * ln_gamma[None, :, None, :] + ln_beta[None, :, None, :]
        b, hh, n, e = out.shape
        return out.transpose(0, 2, 1, 3).reshape(b, n, hh * e)

    x = _layernorm(x + _L0_gnn_ref(x, adj, L0_gnn_W, L0_gnn_a_src, L0_gnn_a_dst, L0_gnn_bias, L0_gnn_ln_gamma, L0_gnn_ln_beta), axis=-1)
    return x


_drawn_inputs = setup_inputs


def setup_inputs(seed=0):
    import zlib

    import numpy as np

    out = dict(_drawn_inputs(seed))
    spreads = {'L0_gnn_bias': (0.0, 0.1), 'L0_gnn_ln_gamma': (1.0, 0.2), 'L0_gnn_ln_beta': (0.0, 0.1)}
    factors = {}
    for name, (base, spread) in spreads.items():
        noise = np.random.default_rng([zlib.crc32(name.encode()), seed]).standard_normal(out[name].shape)
        drawn = base * np.exp(spread * noise) if base else spread * noise
        out[name] = jnp.asarray(drawn.astype(out[name].dtype))
    for name, factor in factors.items():
        out[name] = (out[name] * factor).astype(out[name].dtype)
    return out
```

```python
import numpy as np
from contextlib import ExitStack

import concourse.bass as bass
from concourse import mybir

F32 = mybir.dt.float32
F16 = mybir.dt.float16
BF16 = mybir.dt.bfloat16
F8 = mybir.dt.float8e4
I8 = mybir.dt.int8
U32 = mybir.dt.uint32
I32 = mybir.dt.int32
ALU = mybir.AluOpType
ACT = mybir.ActivationFunctionType
AX = mybir.AxisListType

P = 128
EDGE4 = 0x20202020
NOT_ONE4 = 0xFEFEFEFE
BIG = 2.0 ** 100
QUANTUM = 1.5 * 2.0 ** -40
SCALE = 4096.0
TINY = 2.0 ** -90
SLOPE = 0.01
EPS_HEAD = 1e-6
EPS_OUT = 1e-5
NEG = -1e9
SPAN_LIMIT = 11.0
LOW_LIMIT = 60.0
SIZE_LIMIT = 1e6
H_LIMIT = 15.9

DVE_QUARTERS = (0, 1)

DVE_STEPS = 73
POOL_STEPS = 84
UNIT_STEPS = 28
OUT_STEPS = 4


class Steps:

    def __init__(self, sem):
        self.sem, self.base, self.n = sem, 0, 0

    def rebase(self, base):
        self.base, self.n = base, 0

    def mark(self, ins):
        ins.then_inc(self.sem, 1)
        self.n += 1
        return self.base + self.n

    def after(self, eng, value):
        eng.wait_ge(self.sem, value)

    def chain(self, eng, ins):
        self.after(eng, self.mark(ins))


def wait(eng, sem, value):
    if isinstance(value, int) and value <= 0:
        return
    eng.wait_ge(sem, value)


def adj_resnorm(nc, *tensors):
    with nc.sbuf_tensor("flag", [1, 1], I32) as flag:
        fast_pass(nc, flag, *tensors)
        general_pass(nc, flag, *tensors)


def fast_pass(nc, flag, x, adj, w, a_src, a_dst, bias, gamma, beta, out):
    NB, N, D = x.shape
    H, _, HO = w.shape
    assert (N, D, H, HO) == (2048, 256, 4, 64)
    KB = D // P
    Q = N // 512
    TILES = N // P
    HALF = N // 2
    UNITS = 2 * H
    HT = HALF // P
    E1 = HO + 1
    EX = HO + 2
    WE = H * EX

    ctx = ExitStack()
    with ctx:
        def sb(name, shape, dt):
            return ctx.enter_context(nc.sbuf_tensor(name, shape, dt))

        def psum(name, shape):
            return ctx.enter_context(nc.psum_tensor(name, shape, F32))

        def sem(name):
            return ctx.enter_context(nc.semaphore(name))

        Gm = [sb(f"Gm{i}", [P, Q, HALF, 4], F8) for i in range(2)]
        Lm = [sb(f"Lm{i}", [P, Q, HALF, 4], F8) for i in range(2)]
        Us = [sb(f"Us{i}", [P, HALF, 4], F8) for i in range(2)]
        Mt = [sb(f"Mt{i}", [P, Q, HALF], U32) for i in range(2)]
        Xh = [sb(f"Xh{i}", [P, TILES, 4 * E1], F16) for i in range(H)]
        sB = [sb(f"sB{i}", [P, HALF], F32) for i in range(2)]
        hx = sb("hx", [P, TILES, H, EX], F32)
        ho = [sb(f"ho{i}", [P, HT, H, HO], F32) for i in range(2)]
        stage = [sb(f"stage{i}", [P, N], I8) for i in range(2)]
        xs = sb("xs", [P, 4, D], F32)
        xT = sb("xT", [P, KB, 512], F32)
        accS = [sb(f"accS{i}", [P, 4, 4 * E1], F32) for i in range(2)]
        xr = sb("xr", [P, HT, D], F32)
        We = sb("We", [P, KB, H, EX], F32)
        ident = sb("ident", [P, P], F32)
        ones = sb("ones", [P, P], BF16)
        gammaB = sb("gammaB", [P, D], F32)
        betaB = sb("betaB", [P, D], F32)
        biasB = sb("biasB", [P, H, HO], F32)
        seen = sb("seen", [P, N // 4], U32)
        sd = sb("sd", [P, TILES, H, 2], F32)
        dpos = sb("dpos", [P, H, TILES], F32)
        dneg = sb("dneg", [P, H, TILES], F32)
        dd = sb("dd", [P, H, TILES], F32)
        Bx = sb("Bx", [P, 2, H, TILES], F32)
        sm = sb("sm", [P, H, TILES], F32)
        rAll = sb("rAll", [P, H, TILES], F32)
        rr = [sb(f"rr{i}", [P, H, HT], F32) for i in range(2)]
        pm = sb("pm", [P, 16], F32)
        mx = sb("mx", [16, 1], F32)
        mmb = sb("mmb", [P, 16], F32)
        rdn = sb("rdn", [P, 2, 4], F32)
        st = sb("st", [P, HT * H, 6], F32)
        lnA = sb("lnA", [P, 5, HT * H], F32)
        rs1 = sb("rs1", [P, HT * H], F32)
        st2 = sb("st2", [P, HT, 6], F32)
        mv = sb("mv", [P, HT, 2], F32)
        vv = sb("vv", [P, HT], F32)
        rs2 = sb("rs2", [P, HT], F32)
        mhalf = sb("mhalf", [P, HT * H], F32)
        xsum = sb("xsum", [P, KB, Q], F32)
        xtot = sb("xtot", [P, KB], F32)
        hf = sb("hf", [P, H, E1], F32)
        hpart = sb("hpart", [P, 3, H, E1], BF16)
        hsN = sb("hsN", [P, H, E1], BF16)
        hs = sb("hs", [P, H, E1], BF16)
        viol = sb("viol", [P, 4], F32)
        guard = sb("guard", [P, 16], F32)
        aa = sb("aa", [8, HO], F32)
        aT = sb("aT", [HO, 8], F32)
        Tt = xT[:].rearrange("p k i -> p (k i)")[:, 0:TILES // 2 * E1].rearrange("p (t e) -> p t e", e=E1)
        rowb = [xT[0:8, :, :], xs[0:8, :, :].rearrange("p (k c) d -> p k (c d)", k=2)]

        acc = psum("acc", [P, 4, 512])
        tp = psum("tp", [P, 2, 512])
        hp = psum("hp", [P, 2, 512])

        rows_d = nc.dram_tensor("score_rows", [NB, 2 * H, N], F32).ap()
        mx_d = nc.dram_tensor("score_bounds", [NB, 16], F32).ap()

        const_in = sem("const_in")
        x_in = sem("x_in")
        adj_in = [sem("adj_in0"), sem("adj_in1")]
        sB_in = [sem("sB_in0"), sem("sB_in1")]
        rows_out = sem("rows_out")
        mx_out = sem("mx_out")
        mx_in = sem("mx_in")
        xr_in = sem("xr_in")
        y_out = sem("y_out")
        made = sem("made")
        dset = sem("dset")
        tp_full = sem("tp_full")
        tp_free = sem("tp_free")
        h_full = sem("h_full")
        h_out = sem("h_out")
        acc_full = sem("acc_full")
        acc_free = sem("acc_free")
        u_done = sem("u_done")
        gl_done = sem("gl_done")
        sd_done = sem("sd_done")
        pm_done = sem("pm_done")
        mx_done = sem("mx_done")
        row_done = sem("row_done")
        dd_done = sem("dd_done")
        exp_done = sem("exp_done")
        bx_done = sem("bx_done")
        d_done = sem("d_done")
        xtot_done = sem("xtot_done")
        x_prep = sem("x_prep")
        half_prep = sem("half_prep")
        fin1 = sem("fin1")
        fin2 = sem("fin2")
        var1 = sem("var1")
        rstd1 = sem("rstd1")
        ln1 = sem("ln1")
        res = sem("res")
        var2 = sem("var2")
        rstd2 = sem("rstd2")
        y_done = sem("y_done")
        v_step = sem("v_step")
        p_step = sem("p_step")
        v_cmp = sem("v_cmp")
        hs_done = sem("hs_done")
        scale_done = sem("scale_done")
        settled_at = sem("settled_at")
        flag_in = sem("flag_in")
        flag_sum = sem("flag_sum")
        flag_set = sem("flag_set")

        TP_W, TP_X0, TP_PM0, TP_M0, TP_START, TP_BATCH = 0, 4, 12, 18, 28, 30
        TP_AT = {0: ["m5"], 1: ["m6"], 2: ["m7"], 3: ["x0", "x1", "m8"], 4: ["x2", "x3", "m9"],
                 5: ["pm", "m10"], 6: ["m11"], 7: ["m12"]}
        body_use, at = {}, 0
        for k in range(UNITS):
            for what in TP_AT[k]:
                body_use[what] = at
                at += 6 if what == "pm" else 2
        assert at == TP_BATCH

        def tp_at(b, what):
            if b is None:
                return {"W": TP_W, "x": TP_X0, "pm": TP_PM0, "m": TP_M0}[what[0] if what != "pm" else "pm"] + (
                    2 * int(what[1:]) if what[0] in "xm" and what != "pm" else 0)
            return b * TP_BATCH + (TP_START + body_use[what])

        def row_chunk(b, m, s):
            return one(adj, b)[512 * (m // 2):512 * (m // 2) + 512, :].rearrange("(p c) j -> p c j", c=4)[:, 2 * (m % 2) + s, :]

        def one(t, b):
            if isinstance(b, int):
                return t[b]
            return t[bass.ds(b, 1)].rearrange("o n d -> (o n) d")

        def nodes(t, b, q):
            return one(t, b)[512 * q:512 * q + 512, :].rearrange("(p c) d -> p c d", c=4)

        def words(t):
            return t[:].rearrange("p q i c -> p q (i c)").bitcast(U32)

        def loop_batches(eng, steps, per_batch, batch):
            batch(0, True, NB == 1)
            base = steps.base + steps.n if steps else 0
            if NB > 2:
                with eng.Fori(1, NB - 1) as b:
                    if steps:
                        steps.rebase((b - 1) * per_batch + base)
                    batch(b, False, False)
                    assert not steps or steps.n == per_batch, steps.n
                if steps:
                    steps.rebase(base + (NB - 2) * per_batch)
            if NB > 1:
                batch(NB - 1, False, True)

        def settled(eng):
            eng.sem_inc(settled_at, 1)

        block = ctx.enter_context(nc.Block())

        @block.sync
        def _(sp):
            def load_x(b, j, last_use):
                wait(sp, tp_full, last_use)
                sp.dma_start(xs[:], nodes(x, b, j)).then_inc(x_in, 16)

            def load_scores(b, k, n):
                half, h = k // H, k % H
                wait(sp, u_done, 4 * (n - 1))
                wait(sp, gl_done, 4 * (n - 1))
                src = one(rows_d, b)[2 * h:2 * h + 1, half * HALF:(half + 1) * HALF]
                sp.dma_start(sB[k % 2][:], src.to_broadcast([P, HALF])).then_inc(sB_in[k % 2], 16)

            def bounds_and_rows(b, nb):
                sp.wait_ge(mx_done, nb + 1)
                dst = one_mx(b)
                sp.dma_start(dst.rearrange("o m -> m o"), mx[:]).then_inc(mx_out, 16)
                sp.wait_ge(mx_out, 16 * nb + 16)
                sp.dma_start(mmb[:], one_mx(b).to_broadcast([P, 16])).then_inc(mx_in, 16)
                for r in range(2):
                    sp.wait_ge(row_done, 2 * nb + r + 1)
                    sp.dma_start(one(rows_d, b)[:, r * HALF:(r + 1) * HALF],
                                 rowb[r].rearrange("p k i -> p (k i)")).then_inc(rows_out, 16)
                sp.wait_ge(rows_out, 32 * nb + 32)

            def one_mx(b):
                return mx_d[b:b + 1] if isinstance(b, int) else mx_d[bass.ds(b, 1)]

            def load_res(b, half, n):
                for g in range(2):
                    wait(sp, y_out, 16 * n)
                    sp.dma_start(xr[:, 4 * g:4 * g + 4, :], nodes(x, b, 2 * half + g)).then_inc(xr_in, 16)

            def store_res(b, half, n):
                sp.wait_ge(y_done, n + 1)
                for g in range(2):
                    sp.dma_start(nodes(out, b, 2 * half + g), xr[:, 4 * g:4 * g + 4, :]).then_inc(y_out, 16)

            for kb in range(KB):
                sp.dma_start(We[:, kb, :, 0:HO], w[:, kb * P:(kb + 1) * P, :].rearrange("h p e -> p h e")
                             ).then_inc(const_in, 16)
            sp.dma_start(aa[0:H, :], a_src[:, 0, :]).then_inc(const_in, 16)
            sp.dma_start(aa[H:2 * H, :], a_dst[:, 0, :]).then_inc(const_in, 16)
            for dst, src in ((gammaB[:], gamma), (betaB[:], beta), (biasB[:].rearrange("p h e -> p (h e)"), bias)):
                sp.dma_start(dst, src.rearrange("(o h) e -> o (h e)", o=1).to_broadcast([P, D])).then_inc(const_in, 16)
            load_x(0, 0, 0)
            for j in range(1, Q):
                load_x(0, j, TP_X0 + 2 * j)
            bounds_and_rows(0, 0)
            load_scores(0, 0, 0)
            load_scores(0, 1, 1)

            def batch(b, first, last):
                for k in range(UNITS):
                    n = UNITS * b + k
                    if k == 0 and not first:
                        load_res(b - 1, 1, 4 * b - 2)
                    if k == 3 and not first:
                        store_res(b - 1, 1, 2 * b - 1)
                    if k == 4:
                        load_res(b, 0, 4 * b)
                    if k == 7:
                        store_res(b, 0, 2 * b)
                    if not last and k in (1, 3, 4):
                        for j in {1: (0,), 3: (1,), 4: (2, 3)}[k]:
                            load_x(b + 1, j, tp_at(b, f"x{j - 1}") + 2 if j else (TP_X0 + 8 if first else tp_at(b - 1, "x3") + 2))
                    if not last and k == 5:
                        bounds_and_rows(b + 1, b + 1)
                    if k + 2 < UNITS:
                        load_scores(b, k + 2, n + 2)
                    elif not last:
                        load_scores(b + 1, k + 2 - UNITS, n + 2)

            loop_batches(sp, None, 0, batch)
            load_res(NB - 1, 1, 4 * NB - 2)
            store_res(NB - 1, 1, 2 * NB - 1)
            sp.wait_ge(y_out, 16 * 4 * NB)

        @block.gpsimd
        def _(pool):
            ps = Steps(p_step)

            def load_adj(b, m, taken):
                for i in range(2):
                    wait(pool, tp_free, taken - 1 + i)
                    pool.dma_start(stage[i][:], row_chunk(b, m, i)).then_inc(adj_in[i], 16)

            def prep_operands(b, h, branches=(0, 1)):
                if 0 in branches:
                    pool.wait_ge(bx_done, b + 1)
                    pool.wait_ge(rows_out, 32 * b + 32)
                    wait(pool, acc_full, 4 * (UNITS * b + h - 3))
                    pool.wait_ge(hs_done, b + 1)
                    settled(pool)
                    ps.chain(pool, nc.gpsimd.tensor_scalar(hs[:, h, :], hsN[:, h, :], 1.0, 0.0, ALU.mult, ALU.add))
                G8 = TILES // 2
                for j in branches:
                    for g in range(2):
                        t0 = g * G8
                        ps.chain(pool, nc.gpsimd.tensor_tensor(
                            Tt[:], hx[:, t0:t0 + G8, h, 0:E1],
                            Bx[:, j, h, t0:t0 + G8].unsqueeze(2).to_broadcast([P, G8, E1]), ALU.mult))
                        settled(pool)
                        hi = Xh[h][:, t0:t0 + G8, 2 * E1 * j:2 * E1 * j + E1]
                        ps.chain(pool, nc.gpsimd.tensor_scalar(hi, Tt[:], 1.0, 0.0, ALU.mult, ALU.add))
                        last = nc.gpsimd.tensor_tensor(Xh[h][:, t0:t0 + G8, 2 * E1 * j + E1:2 * E1 * (j + 1)],
                                                       Tt[:], hi, ALU.subtract)
                        if (j, g) != (1, 1):
                            ps.chain(pool, last)
                if 1 in branches:
                    last.then_inc(x_prep, 1)
                    pool.wait_ge(x_prep, H * b + h + 1)

            def prep_half(b, half):
                pool.wait_ge(sd_done, b + 1)
                pool.wait_ge(exp_done, 3 * b + 3)
                wait(pool, res, 2 * b + half - 1)
                settled(pool)
                nc.gpsimd.tensor_scalar(ho[half][:], hx[:, half * HT:(half + 1) * HT, :, 0:HO], 1.0, 0.0,
                                        ALU.mult, ALU.add)
                nc.gpsimd.tensor_scalar(rr[half][:], rAll[:, :, half * HT:(half + 1) * HT], 1.0, 0.0,
                                        ALU.mult, ALU.add).then_inc(half_prep, 1)
                pool.wait_ge(half_prep, 2 * b + half + 1)

            def combine(n, k, g):
                half, h = k // H, k % H
                pool.wait_ge(acc_free, 4 * n + 2 * g + 2)
                a = accS[g][:].rearrange("p t (j s e) -> p t j s e", j=2, s=2)
                hi, lower = a[:, :, :, 0, :], a[:, :, 1, 0, :]
                ps.chain(pool, nc.gpsimd.tensor_tensor(hi, hi, a[:, :, :, 1, :], ALU.add))
                ps.chain(pool, nc.gpsimd.tensor_tensor(
                    lower, lower, rr[half][:, h, 4 * g:4 * g + 4].unsqueeze(2).to_broadcast([P, 4, E1]), ALU.mult))
                nc.gpsimd.tensor_tensor(a[:, :, 0, 0, :], a[:, :, 0, 0, :], lower, ALU.add).then_inc(fin1, 1)
                pool.wait_ge(fin1, 2 * n + g + 1)

            def rstd(n, src, dst, width, src_sem, dst_sem):
                pool.wait_ge(src_sem, n + 1)
                nc.gpsimd.tensor_tensor(dst, src, mhalf[:, 0:width], ALU.pow).then_inc(dst_sem, 1)

            def bc(t):
                return t[:].unsqueeze(1).to_broadcast([P, HT, D])

            def residual_in(n):
                pool.wait_ge(xr_in, 32 * n + 32)
                ps.chain(pool, nc.gpsimd.tensor_tensor(xr[:], xr[:], bc(betaB), ALU.add))

            def residual(half, n):
                hof = ho[half][:].rearrange("p t h e -> p t (h e)")
                pool.wait_ge(ln1, n + 1)
                ps.chain(pool, nc.gpsimd.tensor_tensor(hof, hof, bc(gammaB), ALU.mult))
                nc.gpsimd.tensor_tensor(xr[:], xr[:], hof, ALU.add).then_inc(res, 1)
                pool.wait_ge(res, n + 1)

            nc.gpsimd.memset(ident[:], 0.0)
            ps.chain(pool, nc.gpsimd.memset(mhalf[:], -0.5))
            load_adj(0, 0, 0)
            nc.gpsimd.affine_select(out=ident[:], in_=ident[:], compare_op=ALU.not_equal, fill=1.0,
                                    base=0, pattern=[[-1, P]], channel_multiplier=1).then_inc(made, 1)
            for m in range(1, 3):
                load_adj(0, m, TP_M0 + 2 * m)
            pool.wait_ge(const_in, 16 * 7)
            prep_half(0, 0)
            prep_operands(0, 0)
            for m in range(3, 6):
                load_adj(0, m, TP_M0 + 2 * m)
            prep_operands(0, 1)

            def batch(b, first, last):
                for k in range(UNITS):
                    n = UNITS * b + k
                    if k == 0 and not first:
                        load_adj(b, 5, tp_at(b - 1, "m12") + 2)
                    elif k in (1, 2):
                        load_adj(b, k + 5, tp_at(b, f"m{k + 4}") + 2)
                    elif k > 2 and not last:
                        load_adj(b + 1, k - 3, tp_at(b, f"m{k + 4}") + 2)
                    if not (first and k == 0):
                        combine(n - 1, (k - 1) % UNITS, 1)
                    operands = {0: (b, 2), 2: (b, 3)}.get(k)
                    if k in (6, 7) and not last:
                        operands = (b + 1, k - 6)
                    if operands:
                        prep_operands(*operands, (0,))
                    if k == 1:
                        if not first:
                            residual(1, 2 * b - 1)
                        prep_half(b, 1)
                    if k == 5:
                        residual(0, 2 * b)
                    combine(n, k, 0)
                    if k == 0 and not first:
                        rstd(2 * b - 1, lnA[:, 3, :], rs1[:], HT * H, var1, rstd1)
                        residual_in(2 * b - 1)
                    if k == 2 and not first:
                        rstd(2 * b - 1, vv[:], rs2[:], HT, var2, rstd2)
                    if k == 4:
                        residual_in(2 * b)
                        rstd(2 * b, lnA[:, 3, :], rs1[:], HT * H, var1, rstd1)
                    if k == 6:
                        rstd(2 * b, vv[:], rs2[:], HT, var2, rstd2)
                    if operands:
                        prep_operands(*operands, (1,))
                    if k == 7 and not last:
                        prep_half(b + 1, 0)

            loop_batches(pool, ps, POOL_STEPS, batch)
            n = UNITS * NB
            combine(n - 1, UNITS - 1, 1)
            residual_in(2 * NB - 1)
            rstd(2 * NB - 1, lnA[:, 3, :], rs1[:], HT * H, var1, rstd1)
            residual(1, 2 * NB - 1)
            rstd(2 * NB - 1, vv[:], rs2[:], HT, var2, rstd2)

        @block.scalar
        def _(act):
            def compare(b, k, n, q):
                h = k % H
                if q == 0:
                    act.wait_ge(d_done, b + 1)
                    act.wait_ge(sB_in[k % 2], n_half(b, k) * 16 + 16)
                wait(act, gl_done, 4 * n + q - 1)
                settled(act)
                for c in range(3 if q in DVE_QUARTERS else 4):
                    last = nc.scalar.activation(Us[q % 2][:, :, c], sB[k % 2][:], ACT.Relu,
                                                bias=dpos[:, h, 4 * q + c:4 * q + c + 1], scale=BIG, saturate=False)
                last.then_inc(u_done, 1)

            def n_half(b, k):
                return (UNITS // 2) * b + k // 2

            def take(n, p):
                act.wait_ge(acc_full, 4 * n + p + 1)
                if p % 2 == 0:
                    wait(act, fin2, 2 * n + p // 2 - 1)
                b0 = 2 * p % 4
                nc.scalar.copy(accS[p // 2][:, b0:b0 + 2, :], acc[:, b0:b0 + 2, 0:4 * E1]).then_inc(acc_free, 1)

            def take_h(b, t):
                v = TILES * b + t
                if t == 0:
                    wait(act, x_prep, 4 * b)
                    wait(act, half_prep, 2 * b)
                act.wait_ge(h_full, v + 1)
                nc.scalar.copy(hx[:, t, :, :].rearrange("p h e -> p (h e)"), hp[:, t % 2, 0:WE]).then_inc(h_out, 1)

            def factors(b):
                act.wait_ge(dd_done, b + 1)
                wait(act, x_prep, 4 * b)
                wait(act, half_prep, 2 * b)
                for dst, src, scale in ((Bx[:, 0], dd, 1.0), (Bx[:, 1], dd, SLOPE), (rAll[:], sm, SLOPE - 1.0)):
                    nc.scalar.activation(dst, src[:], ACT.Exp, scale=scale).then_inc(exp_done, 1)

            for t in range(TILES):
                take_h(0, t)
            factors(0)
            for q in range(4):
                compare(0, 0, 0, q)

            def batch(b, first, last):
                for k in range(UNITS):
                    n = UNITS * b + k
                    for q in range(5):
                        if q < 4 and k + 1 < UNITS:
                            compare(b, k + 1, n + 1, q)
                        elif q < 4 and not last:
                            compare(b + 1, 0, n + 1, q)
                        if q > 0:
                            take(n, q - 1)
                        projected = {(3, 2): 0, (4, 1): 1, (4, 3): 2, (5, 1): 3}.get((k, q))
                        if projected is not None and not last:
                            for c in range(4):
                                take_h(b + 1, 4 * projected + c)
                        if q == 2 and not last and k == 6:
                            factors(b + 1)

            loop_batches(act, None, 0, batch)

        @block.tensor
        def _(pe):
            def tp_bank(u):
                wait(pe, tp_free, u - 1)

            def turn_x(b, j, u):
                pe.wait_ge(x_in, 16 * (Q * b + j) + 16)
                for kb in range(KB):
                    tp_bank(u + kb)
                    for c in range(4):
                        last = nc.tensor.transpose(tp[:, kb, c * P:(c + 1) * P], xs[:, c, kb * P:(kb + 1) * P], ident[:])
                    last.then_inc(tp_full, 1)

            def project(b, j, u):
                pe.wait_ge(tp_free, u + 2)
                for c in range(4):
                    v = TILES * b + 4 * j + c
                    wait(pe, h_out, v - 1)
                    for kb in range(KB):
                        last = nc.tensor.matmul(hp[:, c % 2, 0:WE], xT[:, kb, c * P:(c + 1) * P],
                                                We[:, kb, :, :].rearrange("p h e -> p (h e)"),
                                                start=(kb == 0), stop=(kb == KB - 1))
                    last.then_inc(h_full, 1)

            def turn_scores(b, u):
                pe.wait_ge(pm_done, b + 1)
                tp_bank(u)
                nc.tensor.transpose(tp[0:16, 0, 0:P], pm[:], ident[:]).then_inc(tp_full, 1)
                pe.wait_ge(sd_done, b + 1)
                for r in range(4):
                    tp_bank(u + 1 + r)
                    for c in range(4):
                        last = nc.tensor.transpose(tp[0:8, (1 + r) % 2, c * P:(c + 1) * P],
                                                   sd[:, 4 * r + c, :, :].rearrange("p h s -> p (h s)"), ident[:])
                    last.then_inc(tp_full, 1)
                pe.wait_ge(xtot_done, b + 1)
                tp_bank(u + 5)
                for kb in range(KB):
                    last = nc.tensor.matmul(tp[:, 1, 0:WE], xtot[:, kb:kb + 1].to_broadcast([P, P]),
                                            We[:, kb, :, :].rearrange("p h e -> p (h e)"),
                                            start=(kb == 0), stop=(kb == KB - 1))
                last.then_inc(tp_full, 1)

            def turn_adj(b, m, u):
                for i in range(2):
                    pe.wait_ge(adj_in[i], 16 * (8 * b + m) + 16)
                    tp_bank(u + i)
                    for q in range(Q):
                        last = nc.tensor.transpose(tp[:, i, q * P:(q + 1) * P],
                                                   stage[i][:, 512 * q:512 * q + 512].bitcast(F32), ident[:])
                    last.then_inc(tp_full, 1)

            def sums(n, k, t):
                h, buf, bank = k % H, k % 2, t % 4
                for q in range(Q):
                    for c in range(4):
                        first = q == 0 and c == 0
                        nc.tensor.matmul(acc[:, bank, 0:2 * E1], Gm[buf][:, q, t * P:(t + 1) * P, c],
                                         Xh[h][:, 4 * q + c, 0:2 * E1], start=first, stop=False, skip_group_check=True)
                        last = nc.tensor.matmul(acc[:, bank, 2 * E1:4 * E1], Lm[buf][:, q, t * P:(t + 1) * P, c],
                                                Xh[h][:, 4 * q + c, 2 * E1:4 * E1], start=False,
                                                stop=(q == Q - 1 and c == 3), skip_group_check=True)
                        if first:
                            nc.tensor.matmul(acc[:, bank, 0:E1], ones[:], hs[:, h, :], start=False, stop=False,
                                             skip_group_check=True)
                return last

            pe.wait_ge(made, 1)
            pe.wait_ge(const_in, 16 * 7)
            for kb in range(KB):
                for h in range(H):
                    last = nc.tensor.transpose(tp[0:HO, kb, h * P:(h + 1) * P], We[:, kb, h, 0:HO], ident[:])
                last.then_inc(tp_full, 1)
            tp_bank(2)
            nc.tensor.transpose(tp[0:HO, 0, 0:8], aa[:], ident[0:8, 0:8]).then_inc(tp_full, 1)
            pe.wait_ge(tp_free, 3)
            tp_bank(3)
            for kb in range(KB):
                for h in range(H):
                    last = nc.tensor.matmul(tp[:, 1, 2 * (H * kb + h):2 * (H * kb + h) + 2], xT[0:HO, kb, h * P:(h + 1) * P],
                                            aT[:, h:h + H + 1:H], start=True, stop=True)
            last.then_inc(tp_full, 1)
            pe.wait_ge(tp_free, 4)
            for j in range(Q):
                turn_x(0, j, TP_X0 + 2 * j)
                project(0, j, TP_X0 + 2 * j)
            turn_scores(0, TP_PM0)
            pe.wait_ge(dset, 1)
            for chunk in range(5):
                turn_adj(0, chunk, TP_M0 + 2 * chunk)

            def batch(b, first, last):
                for k in range(UNITS):
                    n = UNITS * b + k

                    def beside(p):
                        if not last:
                            turned = {(3, 0): 0, (3, 3): 1, (4, 1): 2, (4, 3): 3}.get((k, p))
                            projected = {(3, 1): 0, (4, 0): 1, (4, 2): 2, (5, 0): 3}.get((k, p))
                            if turned is not None:
                                turn_x(b + 1, turned, tp_at(b, f"x{turned}"))
                            if projected is not None:
                                project(b + 1, projected, tp_at(b, f"x{projected}"))
                        if k == 5 and p == 3 and not last:
                            turn_scores(b + 1, tp_at(b, "pm"))
                        chunk = k + 5
                        if p == (2 if k < 3 or k > 5 else 3) and chunk < 8:
                            turn_adj(b, chunk, tp_at(b, f"m{chunk}"))
                        elif p == (2 if k < 3 or k > 5 else 3) and not last:
                            turn_adj(b + 1, chunk - 8, tp_at(b, f"m{chunk}"))

                    pe.wait_ge(gl_done, 4 * n + 4)
                    if k < H:
                        pe.wait_ge(x_prep, 4 * b + k + 1)
                    for p in range(HT // 2):
                        wait(pe, acc_free, 4 * n + p - 1)
                        settled(pe)
                        sums(n, k, 2 * p)
                        sums(n, k, 2 * p + 1).then_inc(acc_full, 1)
                        beside(p)

            loop_batches(pe, None, 0, batch)
            pe.wait_ge(flag_in, 1)
            nc.tensor.matmul(tp[0:1, 0, 0:1], guard[:, 0:1], guard[:, 1:2], start=True, stop=True).then_inc(flag_sum, 1)

        @block.vector
        def _(dve):
            vs = Steps(v_step)
            V = nc.vector

            def chain(ins):
                vs.chain(dve, ins)

            def n_half(b, k):
                return (UNITS // 2) * b + k // 2

            def take_x(b, j, u):
                wait(dve, h_full, TILES * b + 4 * j)
                if j == 0:
                    wait(dve, x_prep, H * b)
                for kb in range(KB):
                    dve.wait_ge(tp_full, u + kb + 1)
                    V.tensor_scalar(xT[:, kb, :], tp[:, kb, :], 1.0, None, ALU.mult, ALU.add,
                                    accum_out=xsum[:, kb, j:j + 1]).then_inc(tp_free, 1)

            def scores(b):
                dve.wait_ge(h_out, TILES * b + TILES)
                chain(V.tensor_scalar(sd[:], hx[:, :, :, HO:EX], QUANTUM, QUANTUM, ALU.add, ALU.subtract))
                V.tensor_scalar(hx[:, :, :, HO:E1], hx[:, :, :, HO:E1], 0.0, 1.0, ALU.mult, ALU.add
                                ).then_inc(sd_done, 1)
                view = sd[:].rearrange("p t h s -> p (h s) t")
                V.tensor_reduce(pm[:, 0:8], view, AX.X, ALU.max)
                V.tensor_reduce(pm[:, 8:16], view, AX.X, ALU.min, negate=True).then_inc(pm_done, 1)
                V.tensor_reduce(xtot[:], xsum[:], AX.X, ALU.add).then_inc(xtot_done, 1)
                V.tensor_reduce(guard[:, 2:3], hx[:, :, :, 0:HO], AX.XYZ, ALU.max, apply_absolute_value=True)

            def bounds(u):
                dve.wait_ge(tp_full, u + 1)
                V.tensor_reduce(mx[:], tp[0:16, 0, 0:P], AX.X, ALU.max).then_inc(tp_free, 1)
                dve.wait_ge(tp_free, u + 1)
                dve.sem_inc(mx_done, 1)

            def rows(b, u):
                wait(dve, h_full, TILES * b + TILES)
                for r in range(4):
                    dve.wait_ge(tp_full, u + 2 + r)
                    V.tensor_copy(rowb[r // 2][:, r % 2, :], tp[0:8, (1 + r) % 2, :]).then_inc(tp_free, 1)
                    if r % 2:
                        dve.wait_ge(tp_free, u + 2 + r)
                        dve.sem_inc(row_done, 1)

            def mean_parts(b, u):
                dve.wait_ge(tp_full, u + 6)
                V.tensor_scalar(hf[:, :, 0:HO], tp[:, 1, 0:WE].rearrange("p (h e) -> p h e", h=H)[:, :, 0:HO], TINY,
                                None, ALU.mult).then_inc(tp_free, 1)
                dve.wait_ge(tp_free, u + 6)
                chain(V.memset(hf[:, :, HO:E1], N * TINY))
                chain(V.tensor_copy(hpart[:, 0], hf[:]))
                chain(V.tensor_tensor(hf[:], hf[:], hpart[:, 0], ALU.subtract))
                chain(V.tensor_copy(hpart[:, 1], hf[:]))
                chain(V.tensor_tensor(hpart[:, 2], hf[:], hpart[:, 1], ALU.subtract))
                wait(dve, x_prep, H * b)
                chain(V.tensor_scalar(hsN[:], hpart[:, 0], ident[:, 0:1], None, ALU.mult))
                chain(V.scalar_tensor_tensor(hsN[:], hpart[:, 1], ident[:, 1:2], hsN[:], ALU.mult, ALU.add))
                V.scalar_tensor_tensor(hsN[:], hpart[:, 2], ident[:, 2:3], hsN[:], ALU.mult, ALU.add
                                       ).then_inc(hs_done, 1)

            def factors_in(b):
                dve.wait_ge(mx_in, 16 * b + 16)
                wait(dve, exp_done, 3 * b)
                dve.wait_ge(sd_done, b + 1)
                sv = sd[:].rearrange("p t h s -> p s h t")
                bc = mmb[:, 1:8:2].unsqueeze(2).to_broadcast([P, H, TILES])
                V.tensor_tensor(dd[:], sv[:, 1], bc, ALU.subtract)
                V.tensor_tensor(sm[:], sv[:, 0], bc, ALU.add).then_inc(dd_done, 1)
                V.tensor_tensor(guard[:, 4:8], mmb[:, 1:8:2], mmb[:, 9:16:2], ALU.add)
                chain(V.tensor_tensor(guard[:, 8:12], mmb[:, 8:16:2], mmb[:, 1:8:2], ALU.subtract))
                V.tensor_reduce(guard[:, 12:13], guard[:, 4:8], AX.X, ALU.max)
                V.tensor_reduce(guard[:, 13:14], guard[:, 8:12], AX.X, ALU.max)
                chain(V.tensor_reduce(guard[:, 14:15], mmb[:], AX.X, ALU.max))
                V.tensor_tensor(viol[:, 0:3], viol[:, 0:3], guard[:, 12:15], ALU.max)
                chain(V.tensor_tensor(viol[:, 3:4], viol[:, 3:4], guard[:, 2:3], ALU.max))

            def factors_out(b):
                dve.wait_ge(exp_done, 3 * b + 2)
                V.tensor_scalar(Bx[:], Bx[:], SCALE, None, ALU.mult).then_inc(bx_done, 1)

            def operands_d(b):
                wait(dve, u_done, 4 * UNITS * b)
                wait(dve, gl_done, 4 * UNITS * b)
                sv = sd[:].rearrange("p t h s -> p s h t")
                V.tensor_scalar(dpos[:], sv[:, 1], BIG, None, ALU.mult)
                V.tensor_scalar(dneg[:], sv[:, 1], -1.0, None, ALU.mult).then_inc(d_done, 1)

            def take_adj(b, m, u, n_gl):
                half = m // 4
                wait(dve, gl_done, n_gl)
                for i in range(2):
                    dve.wait_ge(adj_in[i], 16 * (8 * b + m) + 16)
                    wait(dve, tp_free, u + i)
                    V.tensor_tensor(seen[:], seen[:], stage[i][:].bitcast(U32), ALU.bitwise_or)
                    at = (2 * (m % 4) + i) * P
                    dve.wait_ge(tp_full, u + i + 1)
                    V.tensor_scalar(Mt[half][:, :, at:at + P], tp[:, i, :].rearrange("p (q i) -> p q i", q=Q).bitcast(U32),
                                    5, EDGE4, ALU.logical_shift_left, ALU.bitwise_and).then_inc(tp_free, 1)

            def compare(b, k, n, q):
                if q not in DVE_QUARTERS:
                    return
                dve.wait_ge(sB_in[k % 2], n_half(b, k) * 16 + 16)
                dve.wait_ge(d_done, b + 1)
                wait(dve, gl_done, 4 * n + q - 1)
                settled(dve)
                V.tensor_scalar(Us[q % 2][:, :, 3], sB[k % 2][:], dneg[:, k % H, 4 * q + 3:4 * q + 4], None,
                                ALU.is_gt, saturate=False).then_inc(v_cmp, 1)

            def masks(k, n, q, tp_done):
                half, buf = k // H, k % 2
                if q == 0:
                    wait(dve, acc_full, 4 * (n - 1))
                    wait(dve, tp_free, tp_done)
                if q in DVE_QUARTERS:
                    dve.wait_ge(v_cmp, len(DVE_QUARTERS) * n + DVE_QUARTERS.index(q) + 1)
                dve.wait_ge(u_done, 4 * n + q + 1)
                u = Us[q % 2][:].rearrange("p i c -> p (i c)").bitcast(U32)
                V.tensor_tensor(words(Gm[buf])[:, q], u, Mt[half][:, q], ALU.bitwise_and)
                V.scalar_tensor_tensor(words(Lm[buf])[:, q], u, 0xFFFFFFFF, Mt[half][:, q], ALU.bitwise_xor,
                                       ALU.bitwise_and).then_inc(gl_done, 1)

            def finish(n, k, g):
                half, h = k // H, k % H
                dve.wait_ge(fin1, 2 * n + g + 1)
                chain(V.reciprocal(rdn[:, g, :], accS[g][:, :, HO]))
                num = accS[g][:, :, 0:HO]
                chain(V.tensor_tensor(num, num, rdn[:, g, :].unsqueeze(2).to_broadcast([P, 4, HO]), ALU.mult))
                chain(V.tensor_tensor(num, num, biasB[:, h, :].unsqueeze(1).to_broadcast([P, 4, HO]), ALU.add))
                dst = ho[half][:, 4 * g:4 * g + 4, h, :]
                V.scalar_tensor_tensor(dst, num, 0.0, dst, ALU.max, ALU.add).then_inc(fin2, 1)

            def head_stats(half, n):
                dve.wait_ge(fin2, 8 * n + 8)
                wait(dve, rstd1, n)
                wait(dve, ln1, n)
                v = ho[half][:].rearrange("p t h e -> p (t h) e")
                for i in range(HT * H):
                    last = V.bn_stats(st[:, i, :], v[:, i, :])
                chain(last)
                V.tensor_tensor(lnA[:, 1, :], st[:, :, 1], st[:, :, 4], ALU.subtract)
                V.tensor_tensor(lnA[:, 2, :], st[:, :, 2], st[:, :, 5], ALU.add)
                chain(V.tensor_tensor(lnA[:, 0, :], st[:, :, 1], st[:, :, 4], ALU.add))
                V.tensor_scalar(lnA[:, 4, :], lnA[:, 0, :], 0.5, None, ALU.mult)
                chain(V.tensor_tensor(lnA[:, 1, :], lnA[:, 1, :], lnA[:, 1, :], ALU.mult))
                chain(V.scalar_tensor_tensor(lnA[:, 2, :], lnA[:, 1, :], HO / 4.0, lnA[:, 2, :], ALU.mult, ALU.add))
                V.tensor_scalar(lnA[:, 3, :], lnA[:, 2, :], 1.0 / HO, EPS_HEAD, ALU.mult, ALU.add).then_inc(var1, 1)

            def head_apply(half, n):
                v = ho[half][:].rearrange("p t h e -> p (t h) e")
                bc = lambda t: t.unsqueeze(2).to_broadcast([P, HT * H, HO])
                dve.wait_ge(var1, n + 1)
                chain(V.tensor_tensor(v, v, bc(lnA[:, 4, :]), ALU.subtract))
                dve.wait_ge(rstd1, n + 1)
                V.tensor_tensor(v, v, bc(rs1[:]), ALU.mult).then_inc(ln1, 1)

            def out_stats(n):
                dve.wait_ge(res, n + 1)
                wait(dve, rstd2, n)
                wait(dve, y_done, n)
                for t in range(HT):
                    last = V.bn_stats(st2[:, t, :], xr[:, t, :])
                chain(last)
                settled(dve)
                for t in range(HT):
                    last = V.bn_aggr(mv[:, t, :], st2[:, t, :])
                chain(last)
                V.tensor_scalar(vv[:], mv[:, :, 1], EPS_OUT, None, ALU.add).then_inc(var2, 1)

            def out_apply(n):
                dve.wait_ge(rstd2, n + 1)
                for t in range(HT):
                    last = V.tensor_scalar(xr[:, t, :], xr[:, t, :], mv[:, t, 0:1], rs2[:, t:t + 1], ALU.subtract, ALU.mult)
                last.then_inc(y_done, 1)

            V.memset(ones[:], 1.0)
            V.memset(seen[:], 0)
            V.memset(viol[:], 0.0)
            V.memset(guard[:], 1.0).then_inc(dset, 1)
            dve.wait_ge(dset, 1)
            dve.wait_ge(made, 1)
            for kb in range(KB):
                dve.wait_ge(tp_full, kb + 1)
                V.tensor_copy(xT[0:HO, kb, :], tp[0:HO, kb, :]).then_inc(tp_free, 1)
            dve.wait_ge(tp_full, 3)
            V.tensor_copy(aT[:], tp[0:HO, 0, 0:8]).then_inc(tp_free, 1)
            dve.wait_ge(tp_full, 4)
            V.tensor_copy(We[:, :, :, HO:EX], tp[:, 1, 0:4 * H].rearrange("p (k h s) -> p k h s", k=KB, h=H)
                          ).then_inc(tp_free, 1)
            for j in range(Q):
                take_x(0, j, TP_X0 + 2 * j)
            scores(0)
            bounds(TP_PM0)
            rows(0, TP_PM0)
            mean_parts(0, TP_PM0)
            for chunk in range(2):
                take_adj(0, chunk, TP_M0 + 2 * chunk, 0)
            factors_in(0)
            operands_d(0)
            factors_out(0)
            for chunk in range(2, 4):
                take_adj(0, chunk, TP_M0 + 2 * chunk, 0)
            for q in range(4):
                compare(0, 0, 0, q)
                masks(0, 0, q, TP_M0 + 8)
            take_adj(0, 4, TP_M0 + 8, 0)

            def batch(b, first, last):
                for k in range(UNITS):
                    n = UNITS * b + k
                    ahead = (b, k + 1) if k + 1 < UNITS else (b + 1, 0)
                    make = k + 1 < UNITS or not last
                    tp_done = tp_at(b, "m7") + 2 if ahead[1] == H else tp_at(b, "m11") + 2 if ahead[1] == 0 else 0

                    def cmp_(q):
                        if make:
                            compare(*ahead, n + 1, q)

                    def msk_(q):
                        if make:
                            masks(ahead[1], n + 1, q, tp_done)

                    def adj_():
                        chunk = k + 5
                        if chunk < 8:
                            take_adj(b, chunk, tp_at(b, f"m{chunk}"), 4 * UNITS * b)
                        elif not last:
                            n_gl = 4 * UNITS * b + (4 * H if chunk < 12 else 4 * UNITS)
                            take_adj(b + 1, chunk - 8, tp_at(b, f"m{chunk}"), n_gl)

                    if k == 7 and not last:
                        operands_d(b + 1)
                    cmp_(0)
                    cmp_(1)
                    if k == 6 and not last:
                        factors_in(b + 1)
                    msk_(0)
                    if not (first and k == 0):
                        finish(n - 1, (k - 1) % UNITS, 0)
                    cmp_(2)
                    if k == 3 and not last:
                        take_x(b + 1, 0, tp_at(b, "x0"))
                    if k == 3 and not first:
                        out_apply(2 * b - 1)
                    if k == 7:
                        out_apply(2 * b)
                    msk_(1)
                    cmp_(3)
                    if not (first and k == 0):
                        finish(n - 1, (k - 1) % UNITS, 1)
                    if k == 4 and not last:
                        take_x(b + 1, 2, tp_at(b, "x2"))
                    if k == 5 and not last:
                        scores(b + 1)
                    if k == 0 and not first:
                        head_stats(1, 2 * b - 1)
                    if k == 1 and not first:
                        head_apply(1, 2 * b - 1)
                    if k == 2 and not first:
                        out_stats(2 * b - 1)
                    msk_(2)
                    if k == 4:
                        head_stats(0, 2 * b)
                    if k == 5:
                        head_apply(0, 2 * b)
                    if k == 6:
                        out_stats(2 * b)
                    if k == 6 and not last:
                        factors_out(b + 1)
                    if k not in (3, 4, 5):
                        adj_()
                    msk_(3)
                    if k in (3, 4) and not last:
                        take_x(b + 1, 2 * k - 5, tp_at(b, f"x{2 * k - 5}"))
                    if k == 5 and not last:
                        u = tp_at(b, "pm")
                        bounds(u)
                        rows(b + 1, u)
                        mean_parts(b + 1, u)
                    if k in (3, 4, 5):
                        adj_()

            loop_batches(dve, vs, DVE_STEPS, batch)
            finish(UNITS * NB - 1, UNITS - 1, 0)
            finish(UNITS * NB - 1, UNITS - 1, 1)
            head_stats(1, 2 * NB - 1)
            head_apply(1, 2 * NB - 1)
            out_stats(2 * NB - 1)
            out_apply(2 * NB - 1)

            chain(V.tensor_scalar(seen[:], seen[:], NOT_ONE4, None, ALU.bitwise_and))
            chain(V.tensor_reduce(guard[:, 3:4], seen[:], AX.X, ALU.max))
            chain(V.tensor_scalar(guard[:, 3:4], guard[:, 3:4], 0.0, None, ALU.is_gt))
            for i, limit in enumerate((SPAN_LIMIT, LOW_LIMIT, SIZE_LIMIT, H_LIMIT)):
                last = V.tensor_scalar(viol[:, i:i + 1], viol[:, i:i + 1], limit, None, ALU.is_gt)
            chain(last)
            chain(V.tensor_reduce(guard[:, 0:1], viol[:], AX.X, ALU.max))
            V.tensor_tensor(guard[:, 0:1], guard[:, 0:1], guard[:, 3:4], ALU.max).then_inc(flag_in, 1)
            dve.wait_ge(flag_sum, 1)
            V.tensor_copy(flag[:], tp[0:1, 0, 0:1]).then_inc(flag_set, 1)

def general_pass(nc, flag, x, adj, w, a_src, a_dst, bias, gamma, beta, out):
    NB, N, D = x.shape
    H, _, HO = w.shape
    TY = a_src.shape[1]
    KB = D // P
    TILES = N // P
    ES = 2 * TY
    SC = H * ES

    ctx = ExitStack()
    with ctx:
        def sb(name, shape, dt=F32):
            return ctx.enter_context(nc.sbuf_tensor("g_" + name, shape, dt))

        def psum(name, shape):
            return ctx.enter_context(nc.psum_tensor("g_" + name, shape, F32))

        def sem(name):
            return ctx.enter_context(nc.semaphore("g_" + name))

        hx = sb("hx", [P, TILES, H, HO])
        ho = sb("ho", [P, TILES, D])
        sc = sb("sc", [P, TILES, SC])
        rows = sb("rows", [SC, N])
        dB = sb("dB", [P, TY, N])
        adjI = sb("adjI", [P, N], I32)
        adjF = sb("adjF", [P, N])
        wt = sb("wt", [P, N])
        part = sb("part", [P, N])
        prob = sb("prob", [P, N])
        probT = sb("probT", [P, N])
        xin = sb("xin", [P, D])
        xT = sb("xT", [P, KB, P])
        Wf = sb("Wf", [P, KB, H, HO])
        Ws = sb("Ws", [P, KB, SC])
        wT = sb("wT", [HO, KB, H * P])
        aa = sb("aa", [SC, HO])
        aT = sb("aT", [HO, SC])
        ident = sb("ident", [P, P])
        gammaB = sb("gammaB", [P, D])
        betaB = sb("betaB", [P, D])
        biasB = sb("biasB", [P, D])
        mhalf = sb("mhalf", [P, 1])
        es = sb("es", [P, TY])
        nmax = sb("nmax", [P, 1])
        den = sb("den", [P, 1])
        o = sb("o", [P, HO])
        y = sb("y", [P, D])
        st = sb("st", [P, 6])
        mv = sb("mv", [P, 2])
        vv = sb("vv", [P, 1])
        rs = sb("rs", [P, 1])
        tr = psum("tr", [P, 4, 512])
        pr = psum("pr", [P, 2, 512])
        ao = psum("ao", [P, 512])
        rows_d = nc.dram_tensor("all_score_rows", [SC, N], F32).ap()

        const_in, x_in, adj_in, ed_in, xr_in = (sem(n) for n in ("const_in", "x_in", "adj_in", "ed_in", "xr_in"))
        rows_out, y_out = sem("rows_out"), sem("y_out")
        made = sem("made")
        w_turned = sem("w_turned")
        w_taken = sem("w_taken")
        we_full = sem("we_full")
        we_done = sem("we_done")
        x_turned = sem("x_turned")
        xT_done = sem("xT_done")
        h_full = sem("h_full")
        h_taken = sem("h_taken")
        adj_taken = sem("adj_taken")
        w_done = sem("w_done")
        p_done = sem("p_done")
        pt_full = sem("pt_full")
        pt_out = sem("pt_out")
        o_full = sem("o_full")
        var_done, rs_done = sem("var_done"), sem("rs_done")
        var2_done, rs2_done = sem("var2_done"), sem("rs2_done")
        y_done = sem("y_done")
        start_step, unit_step, out_step = sem("start_step"), sem("unit_step"), sem("out_step")
        rows_free = sem("rows_free")
        settled_at = sem("settled_at")

        def settled(eng):
            eng.sem_inc(settled_at, 1)

        def tile_of(t, b, r):
            return t.rearrange("b n d -> (b n) d")[bass.ds(b * N + r * P, P)]

        def units(eng, b, unit):
            for h in range(H):
                with eng.Fori(0, TILES) as r:
                    unit(b * (H * TILES) + (r + h * TILES), h, r)

        block = ctx.enter_context(nc.Block())

        @block.sync
        def _(sp):
            with sp.If(sp.value_load(flag[0:1, 0:1]) != 0):
                for kb in range(KB):
                    sp.dma_start(Wf[:, kb], w[:, kb * P:(kb + 1) * P, :].rearrange("h p e -> p h e")
                                 ).then_inc(const_in, 16)
                for h in range(H):
                    for s, a in enumerate((a_src, a_dst)):
                        at = h * ES + s * TY
                        sp.dma_start(aa[at:at + TY, :], a[h]).then_inc(const_in, 16)
                for dst, src in ((gammaB, gamma), (betaB, beta), (biasB, bias)):
                    sp.dma_start(dst[:], src.rearrange("(o h) e -> o (h e)", o=1).to_broadcast([P, D])
                                 ).then_inc(const_in, 16)
                sp.sem_inc(rows_free, 1)
                with sp.Fori(0, NB) as b:
                    with sp.Fori(0, TILES) as t:
                        v = b * TILES + t
                        sp.wait_ge(x_turned, v + 1)
                        settled(sp)
                        sp.dma_start(xin[:], tile_of(x, b, t)).then_inc(x_in, 16)
                    sp.wait_ge(h_taken, (b + 1) * TILES + 1)
                    sp.dma_start(rows_d, rows[:]).then_inc(rows_out, 16)
                    sp.wait_ge(rows_out, (b + 1) * 16)
                    sp.sem_inc(rows_free, 1)
                    for h in range(H):
                        sp.wait_ge(w_done, b * (H * TILES) + (h * TILES + 1))
                        src = rows_d[h * ES + TY:(h + 1) * ES].rearrange("(o t) n -> o (t n)", o=1)
                        sp.dma_start(dB[:].rearrange("p t n -> p (t n)"), src.to_broadcast([P, TY * N])).then_inc(ed_in, 16)
                        with sp.Fori(0, TILES) as r:
                            sp.wait_ge(adj_taken, b * (H * TILES) + (r + h * TILES) + 1)
                            settled(sp)
                            sp.dma_start(adjI[:], tile_of(adj, b, r)).then_inc(adj_in, 16)
                    with sp.Fori(0, TILES) as r:
                        v = b * TILES + r
                        sp.wait_ge(x_turned, (b + 1) * TILES + 1)
                        settled(sp)
                        sp.dma_start(xin[:], tile_of(x, b, r)).then_inc(xr_in, 16)
                        sp.wait_ge(y_done, v + 1)
                        settled(sp)
                        sp.dma_start(tile_of(out, b, r), y[:]).then_inc(y_out, 16)
                        sp.wait_ge(y_out, (v + 1) * 16)
                        settled(sp)
                sp.wait_ge(y_out, NB * TILES * 16)
            sp.nop()

        @block.gpsimd
        def _(pool):
            with pool.If(pool.value_load(flag[0:1, 0:1]) != 0):
                nc.gpsimd.memset(ident[:], 0.0)
                nc.gpsimd.memset(mhalf[:], -0.5).then_inc(start_step, 1)
                pool.wait_ge(start_step, 1)
                nc.gpsimd.affine_select(out=ident[:], in_=ident[:], compare_op=ALU.not_equal, fill=1.0,
                                        base=0, pattern=[[-1, P]], channel_multiplier=1).then_inc(made, 1)
                pool.wait_ge(made, 1)

                def rstd(index, src_sem, dst_sem):
                    pool.wait_ge(src_sem, index + 1)
                    nc.gpsimd.tensor_tensor(rs[:], vv[:], mhalf[:], ALU.pow).then_inc(dst_sem, 1)

                with pool.Fori(0, NB) as b:
                    units(pool, b, lambda u, h, r: rstd(u, var_done, rs_done))
                    with pool.Fori(0, TILES) as r:
                        rstd(b * TILES + r, var2_done, rs2_done)
            pool.nop()

        @block.scalar
        def _(act):
            with act.If(act.value_load(flag[0:1, 0:1]) != 0):
                def unit(u, h, r):
                    act.wait_ge(w_done, u + 2)
                    nc.scalar.activation(prob[:], wt[:], ACT.Exp, bias=nmax[:, 0:1], scale=1.0,
                                         accum_out=den[:, 0:1]).then_inc(p_done, 1)
                    act.wait_ge(pt_full, u + 1)
                    nc.scalar.copy(probT[:], tr[:].rearrange("p b i -> p (b i)")).then_inc(pt_out, 1)

                with act.Fori(0, NB) as b:
                    units(act, b, unit)
            act.nop()

        @block.tensor
        def _(pe):
            with pe.If(pe.value_load(flag[0:1, 0:1]) != 0):
                pe.sem_inc(x_turned, 1)
                pe.wait_ge(made, 1)
                pe.wait_ge(const_in, 16 * (KB + 2 * H + 3))
                for kb in range(KB):
                    for h in range(H):
                        nc.tensor.transpose(tr[0:HO, kb, h * P:(h + 1) * P], Wf[:, kb, h, :], ident[:])
                nc.tensor.transpose(tr[0:HO, KB, 0:SC], aa[:], ident[0:SC, 0:SC]).then_inc(w_turned, 1)
                pe.wait_ge(w_taken, 1)
                for kb in range(KB):
                    for h in range(H):
                        at = kb * SC + h * ES
                        last = nc.tensor.matmul(pr[:, 0, at:at + ES], wT[:, kb, h * P:(h + 1) * P],
                                                aT[:, h * ES:(h + 1) * ES], start=True, stop=True)
                last.then_inc(we_full, 1)
                pe.wait_ge(we_done, 1)

                def project(v):
                    pe.wait_ge(x_in, (v + 1) * 16)
                    for kb in range(KB):
                        last = nc.tensor.transpose(tr[:, 0, kb * P:(kb + 1) * P], xin[:, kb * P:(kb + 1) * P], ident[:])
                    last.then_inc(x_turned, 1)
                    pe.wait_ge(xT_done, v + 1)
                    for kb in range(KB):
                        flags = dict(start=(kb == 0), stop=(kb == KB - 1))
                        nc.tensor.matmul(pr[:, 0, 0:D], xT[:, kb], Wf[:, kb].rearrange("p h e -> p (h e)"), **flags)
                    for kb in range(KB):
                        flags = dict(start=(kb == 0), stop=(kb == KB - 1))
                        nc.tensor.matmul(pr[:, 1, 0:SC], xT[:, kb], Ws[:, kb], **flags)
                    for kb in range(KB):
                        flags = dict(start=(kb == 0), stop=(kb == KB - 1))
                        last = nc.tensor.matmul(ao[0:SC, 0:P], Ws[:, kb], xT[:, kb], **flags)
                    last.then_inc(h_full, 1)

                def unit(u, h, r):
                    pe.wait_ge(p_done, u + 1)
                    for t in range(TILES):
                        last = nc.tensor.transpose(tr[:, t // 4, t % 4 * P:(t % 4 + 1) * P], prob[:, t * P:(t + 1) * P], ident[:])
                    last.then_inc(pt_full, 1)
                    pe.wait_ge(pt_out, u + 1)
                    for t in range(TILES):
                        last = nc.tensor.matmul(ao[:, 0:HO], probT[:, t * P:(t + 1) * P], hx[:, t, h, :],
                                                start=(t == 0), stop=(t == TILES - 1))
                    last.then_inc(o_full, 1)

                with pe.Fori(0, NB) as b:
                    with pe.Fori(0, TILES) as t:
                        pe.wait_ge(h_taken, b * TILES + t + 1)
                        project(b * TILES + t)
                    units(pe, b, unit)
            pe.nop()

        @block.vector
        def _(dve):
            V = nc.vector
            with dve.If(dve.value_load(flag[0:1, 0:1]) != 0):
                for s in (h_taken, w_done, adj_taken):
                    dve.sem_inc(s, 1)
                dve.wait_ge(w_turned, 1)
                V.tensor_copy(aT[:], tr[0:HO, KB, 0:SC])
                V.tensor_copy(wT[:], tr[0:HO, 0:KB, :]).then_inc(w_taken, 1)
                dve.wait_ge(we_full, 1)
                V.tensor_copy(Ws[:], pr[:, 0, 0:KB * SC].rearrange("p (k s) -> p k s", k=KB)).then_inc(we_done, 1)

                def norm(s, t, width, eps, index, var_sem, rs_sem):
                    s.chain(dve, V.bn_stats(st[:], t[:]))
                    settled(dve)
                    s.chain(dve, V.bn_aggr(mv[:], st[:]))
                    V.tensor_scalar(vv[:], mv[:, 1:2], eps, None, ALU.add).then_inc(var_sem, 1)
                    dve.wait_ge(rs_sem, index + 1)
                    s.chain(dve, V.tensor_scalar(t[:], t[:], mv[:, 0:1], rs[:, 0:1], ALU.subtract, ALU.mult))

                def unit(s, u, h, r):
                    dve.wait_ge(adj_in, (u + 1) * 16)
                    V.tensor_copy(adjF[:], adjI[:]).then_inc(adj_taken, 1)
                    s.chain(dve, V.tensor_copy(es[:], sc[:, bass.ds(r, 1), h * ES:h * ES + TY].rearrange("p o t -> p (o t)")))
                    dve.wait_ge(adj_taken, u + 2)
                    for t in range(TY):
                        to = wt if t == 0 else part
                        s.chain(dve, V.tensor_scalar(part[:], dB[:, t, :], es[:, t:t + 1], None, ALU.add))
                        s.chain(dve, V.scalar_tensor_tensor(to[:], adjF[:], t + 1.0, part[:], ALU.is_equal, ALU.mult))
                        if t:
                            s.chain(dve, V.tensor_tensor(wt[:], wt[:], part[:], ALU.add))
                    s.chain(dve, V.scalar_tensor_tensor(wt[:], wt[:], SLOPE, wt[:], ALU.mult, ALU.max))
                    s.chain(dve, V.tensor_scalar(part[:], adjF[:], 0.0, NEG, ALU.is_equal, ALU.mult))
                    s.chain(dve, V.tensor_tensor(wt[:], wt[:], part[:], ALU.add))
                    V.tensor_reduce(nmax[:], wt[:], AX.X, ALU.max, negate=True).then_inc(w_done, 1)
                    dve.wait_ge(o_full, u + 1)
                    s.chain(dve, V.reciprocal(den[:], den[:]))
                    s.chain(dve, V.tensor_scalar(o[:], ao[:, 0:HO], den[:, 0:1], None, ALU.mult))
                    s.chain(dve, V.tensor_tensor(o[:], o[:], biasB[:, h * HO:(h + 1) * HO], ALU.add))
                    s.chain(dve, V.tensor_scalar(o[:], o[:], 0.0, None, ALU.max))
                    own = hx[:, bass.ds(r, 1), h, :].rearrange("p o e -> p (o e)")
                    s.chain(dve, V.tensor_tensor(o[:], o[:], own, ALU.add))
                    norm(s, o, HO, EPS_HEAD, u, var_done, rs_done)
                    s.chain(dve, V.tensor_tensor(o[:], o[:], gammaB[:, h * HO:(h + 1) * HO], ALU.mult))
                    dst = ho[:, bass.ds(r, 1), h * HO:(h + 1) * HO].rearrange("p o e -> p (o e)")
                    s.chain(dve, V.tensor_tensor(dst, o[:], betaB[:, h * HO:(h + 1) * HO], ALU.add))
                    assert s.n == UNIT_STEPS, s.n

                with dve.Fori(0, NB) as b:
                    dve.wait_ge(rows_free, b + 1)
                    settled(dve)
                    with dve.Fori(0, TILES) as t:
                        v = b * TILES + t
                        dve.wait_ge(x_turned, v + 2)
                        V.tensor_copy(xT[:], tr[:, 0, 0:D].rearrange("p (k i) -> p k i", k=KB)).then_inc(xT_done, 1)
                        dve.wait_ge(h_full, v + 1)
                        settled(dve)
                        V.tensor_copy(hx[:, bass.ds(t, 1)], pr[:, 0:1, 0:D].rearrange("p o (h e) -> p o h e", h=H))
                        V.tensor_copy(sc[:, bass.ds(t, 1)], pr[:, 1:2, 0:SC])
                        V.tensor_copy(rows[:, bass.ds(t * P, P)], ao[0:SC, 0:P]).then_inc(h_taken, 1)
                    dve.wait_ge(h_taken, (b + 1) * TILES + 1)
                    for h in range(H):
                        dve.wait_ge(ed_in, b * (16 * H) + 16 * (h + 1))
                        settled(dve)
                        with dve.Fori(0, TILES) as r:
                            s = Steps(unit_step)
                            u = b * (H * TILES) + (r + h * TILES)
                            s.rebase(u * UNIT_STEPS)
                            unit(s, u, h, r)
                    with dve.Fori(0, TILES) as r:
                        v = b * TILES + r
                        s = Steps(out_step)
                        s.rebase(v * OUT_STEPS)
                        dve.wait_ge(xr_in, (v + 1) * 16)
                        hr = ho[:, bass.ds(r, 1), :].rearrange("p o d -> p (o d)")
                        s.chain(dve, V.tensor_tensor(y[:], xin[:], hr, ALU.add))
                        norm(s, y, D, EPS_OUT, v, var2_done, rs2_done)
                        assert s.n == OUT_STEPS, s.n
                        dve.sem_inc(y_done, 1)
            dve.nop()


_INS = ["x", "adj", "L0_gnn_W", "L0_gnn_a_src", "L0_gnn_a_dst", "L0_gnn_bias", "L0_gnn_ln_gamma", "L0_gnn_ln_beta"]


def kernel(**inputs):
    import numpy as _np
    import concourse.bacc as _bacc
    from concourse import mybir as _mybir
    from concourse.bass_utils import run_bass_kernel_spmd as _run

    nc = _bacc.Bacc("TRN2", target_bir_lowering=False, num_devices=1, dynamic_dma_scratch_size=1024)
    arrays, args = {}, []
    for name in _INS:
        a = _np.ascontiguousarray(inputs[name])
        arrays[f"in_{name}_dram"] = a
        args.append(nc.dram_tensor(f"in_{name}_dram", a.shape, _mybir.dt.from_np(a.dtype), kind="ExternalInput").ap())
    out = nc.dram_tensor("out_0_dram", inputs["x"].shape, _mybir.dt.float32, kind="ExternalOutput").ap()
    adj_resnorm(nc, *args, out)
    r = _run(nc, [arrays], core_ids=[0])
    return r.results[0]["out_0_dram"]
```

```python
import numpy as np
from contextlib import ExitStack

import concourse.bass as bass
from concourse import mybir

F32 = mybir.dt.float32
F16 = mybir.dt.float16
BF16 = mybir.dt.bfloat16
F8 = mybir.dt.float8e4
I8 = mybir.dt.int8
U32 = mybir.dt.uint32
I32 = mybir.dt.int32
ALU = mybir.AluOpType
ACT = mybir.ActivationFunctionType
AX = mybir.AxisListType

P = 128
EDGE4 = 0x20202020
NOT_ONE4 = 0xFEFEFEFE
BIG = 2.0 ** 100
QUANTUM = 1.5 * 2.0 ** -40
SCALE = 4096.0
TINY = 2.0 ** -90
SLOPE = 0.01
EPS_HEAD = 1e-6
EPS_OUT = 1e-5
NEG = -1e9
SPAN_LIMIT = 11.0
LOW_LIMIT = 60.0
SIZE_LIMIT = 1e6
H_LIMIT = 15.9

DVE_QUARTERS = (0,)

DVE_STEPS = 79
POOL_STEPS = 84
UNIT_STEPS = 28
OUT_STEPS = 4


class Steps:

    def __init__(self, sem):
        self.sem, self.base, self.n = sem, 0, 0

    def rebase(self, base):
        self.base, self.n = base, 0

    def mark(self, ins):
        ins.then_inc(self.sem, 1)
        self.n += 1
        return self.base + self.n

    def after(self, eng, value):
        eng.wait_ge(self.sem, value)

    def chain(self, eng, ins):
        self.after(eng, self.mark(ins))


def wait(eng, sem, value):
    if isinstance(value, int) and value <= 0:
        return
    eng.wait_ge(sem, value)


def adj_resnorm(nc, *tensors):
    with nc.sbuf_tensor("flag", [1, 1], I32) as flag:
        fast_pass(nc, flag, *tensors)
        general_pass(nc, flag, *tensors)


def fast_pass(nc, flag, x, adj, w, a_src, a_dst, bias, gamma, beta, out):
    NB, N, D = x.shape
    H, _, HO = w.shape
    assert (N, D, H, HO) == (2048, 256, 4, 64)
    KB = D // P
    Q = N // 512
    TILES = N // P
    HALF = N // 2
    UNITS = 2 * H
    HT = HALF // P
    E1 = HO + 1
    EX = HO + 2
    WE = H * EX

    ctx = ExitStack()
    with ctx:
        def sb(name, shape, dt):
            return ctx.enter_context(nc.sbuf_tensor(name, shape, dt))

        def psum(name, shape):
            return ctx.enter_context(nc.psum_tensor(name, shape, F32))

        def sem(name):
            return ctx.enter_context(nc.semaphore(name))

        Gm = [sb(f"Gm{i}", [P, Q, HALF, 4], F8) for i in range(2)]
        Lm = [sb(f"Lm{i}", [P, Q, HALF, 4], F8) for i in range(2)]
        Us = [sb(f"Us{i}", [P, HALF, 4], F8) for i in range(2)]
        Mt = [sb(f"Mt{i}", [P, Q, HALF], U32) for i in range(2)]
        Xh = [sb(f"Xh{i}", [P, TILES, 4 * E1], F16) for i in range(H)]
        sB = [sb(f"sB{i}", [P, HALF], F32) for i in range(2)]
        hx = [sb(f"hx{i}", [P, TILES, H, EX], F32) for i in range(2)]
        stage = [sb(f"stage{i}", [P, N], I8) for i in range(2)]
        xs = sb("xs", [P, 4, D], F32)
        xT = sb("xT", [P, KB, 512], F32)
        accS = [sb(f"accS{i}", [P, 4, 4 * E1], F32) for i in range(2)]
        xr = sb("xr", [P, HT, D], F32)
        We = sb("We", [P, KB, H, EX], F32)
        ident = sb("ident", [P, P], F32)
        ones = sb("ones", [P, P], BF16)
        gammaB = sb("gammaB", [P, D], F32)
        betaB = sb("betaB", [P, D], F32)
        biasB = sb("biasB", [P, H, HO], F32)
        seen = sb("seen", [P, N // 4], U32)
        sd = sb("sd", [P, TILES, H, 2], F32)
        dpos = sb("dpos", [P, H, TILES], F32)
        dneg = sb("dneg", [P, H, TILES], F32)
        dd = sb("dd", [P, H, TILES], F32)
        Bx = sb("Bx", [P, 2, H, TILES], F32)
        sm = sb("sm", [P, H, TILES], F32)
        rowf = [sb(f"rowf{i}", [P, H, TILES], F32) for i in range(2)]
        pm = sb("pm", [P, 16], F32)
        mx = sb("mx", [16, 1], F32)
        mmb = sb("mmb", [P, 16], F32)
        rdn = sb("rdn", [P, 2, 4], F32)
        st = sb("st", [P, HT * H, 6], F32)
        lnA = sb("lnA", [P, 5, HT * H], F32)
        rs1 = sb("rs1", [P, HT * H], F32)
        st2 = sb("st2", [P, HT, 6], F32)
        mv = sb("mv", [P, HT, 2], F32)
        vv = sb("vv", [P, HT], F32)
        rs2 = sb("rs2", [P, HT], F32)
        xsum = sb("xsum", [P, KB, Q], F32)
        xtot = sb("xtot", [P, KB], F32)
        hf = sb("hf", [P, H, E1], F32)
        hpart = sb("hpart", [P, 3, H, E1], BF16)
        hsN = sb("hsN", [P, H, E1], BF16)
        hs = sb("hs", [P, H, E1], BF16)
        viol = sb("viol", [P, 4], F32)
        guard = sb("guard", [P, 16], F32)
        aa = sb("aa", [8, HO], F32)
        aT = sb("aT", [HO, 8], F32)
        Tt = xT[:].rearrange("p k i -> p (k i)")[:, 0:TILES // 2 * E1].rearrange("p (t e) -> p t e", e=E1)
        rowb = [xT[0:8, :, :], xs[0:8, :, :].rearrange("p (k c) d -> p k (c d)", k=2)]

        acc = psum("acc", [P, 4, 512])
        tp = psum("tp", [P, 2, 512])
        hp = psum("hp", [P, 2, 512])

        rows_d = nc.dram_tensor("score_rows", [NB, 2 * H, N], F32).ap()
        mx_d = nc.dram_tensor("score_bounds", [NB, 16], F32).ap()

        const_in = sem("const_in")
        x_in = sem("x_in")
        adj_in = [sem("adj_in0"), sem("adj_in1")]
        sB_in = [sem("sB_in0"), sem("sB_in1")]
        rows_out = sem("rows_out")
        mx_out = sem("mx_out")
        mx_in = sem("mx_in")
        xr_in = sem("xr_in")
        y_out = sem("y_out")
        made = sem("made")
        dset = sem("dset")
        tp_full = sem("tp_full")
        tp_free = sem("tp_free")
        h_full = sem("h_full")
        h_out = sem("h_out")
        acc_full = sem("acc_full")
        acc_free = sem("acc_free")
        u_done = sem("u_done")
        gl_done = sem("gl_done")
        sd_done = sem("sd_done")
        pm_done = sem("pm_done")
        mx_done = sem("mx_done")
        row_done = sem("row_done")
        dd_done = sem("dd_done")
        exp_done = sem("exp_done")
        bx_done = sem("bx_done")
        d_done = sem("d_done")
        xtot_done = sem("xtot_done")
        x_prep = sem("x_prep")
        fin1 = sem("fin1")
        fin2 = sem("fin2")
        var1 = sem("var1")
        std1 = sem("std1")
        ln1 = sem("ln1")
        res = sem("res")
        var2 = sem("var2")
        std2 = sem("std2")
        y_done = sem("y_done")
        v_step = sem("v_step")
        p_step = sem("p_step")
        v_cmp = sem("v_cmp")
        hs_done = sem("hs_done")
        settled_at = sem("settled_at")
        flag_in = sem("flag_in")
        flag_sum = sem("flag_sum")
        flag_set = sem("flag_set")

        TP_X0, TP_PM0, TP_START, TP_BATCH = 4, 20, 28, 30
        TP_AT = {0: ["m5"], 1: ["m6", "x0"], 2: ["m7", "x1", "x2"], 3: ["x3", "m8"], 4: ["pm", "m9"],
                 5: ["m10"], 6: ["m11"], 7: ["m12"]}
        body_use, at = {}, 0
        for k in range(UNITS):
            for what in TP_AT[k]:
                body_use[what] = at
                at += 6 if what == "pm" else 2
        assert at == TP_BATCH

        def start_x(j):
            return TP_X0 + 4 * j

        def start_m(m):
            return TP_X0 + 2 + 4 * m if m < 4 else TP_START - 2

        def tp_at(b, what, last=False):
            return b * TP_BATCH + (TP_START + body_use[what] - (2 if last and what == "m7" else 0))

        def row_chunk(b, m, s):
            return one(adj, b)[512 * (m // 2):512 * (m // 2) + 512, :].rearrange("(p c) j -> p c j", c=4)[:, 2 * (m % 2) + s, :]

        def one(t, b):
            if isinstance(b, int):
                return t[b]
            return t[bass.ds(b, 1)].rearrange("o n d -> (o n) d")

        def nodes(t, b, q):
            return one(t, b)[512 * q:512 * q + 512, :].rearrange("(p c) d -> p c d", c=4)

        def words(t):
            return t[:].rearrange("p q i c -> p q (i c)").bitcast(U32)

        def loop_batches(eng, steps, per_batch, batch):
            batch(0, 0, True, NB == 1)
            base = steps.base + steps.n if steps else 0
            pairs = (NB - 2) // 2
            assert NB % 2 == 0
            if pairs:
                with eng.Fori(0, pairs) as j:
                    for i in range(2):
                        if steps:
                            steps.rebase((2 * j + i) * per_batch + base)
                        batch(2 * j + (1 + i), (1 + i) % 2, False, False)
                        assert not steps or steps.n == per_batch, steps.n
                if steps:
                    steps.rebase(base + (NB - 2) * per_batch)
            batch(NB - 1, (NB - 1) % 2, False, True)

        def settled(eng):
            eng.sem_inc(settled_at, 1)

        block = ctx.enter_context(nc.Block())

        @block.sync
        def _(sp):
            def load_x(b, j, last_use):
                wait(sp, tp_full, last_use)
                sp.dma_start(xs[:], nodes(x, b, j)).then_inc(x_in, 16)

            def load_scores(b, k, n):
                half, h = k // H, k % H
                wait(sp, u_done, 4 * (n - 1))
                wait(sp, gl_done, 4 * (n - 1))
                src = one(rows_d, b)[2 * h:2 * h + 1, half * HALF:(half + 1) * HALF]
                sp.dma_start(sB[k % 2][:], src.to_broadcast([P, HALF])).then_inc(sB_in[k % 2], 16)

            def bounds_and_rows(b, nb):
                sp.wait_ge(mx_done, nb + 1)
                dst = one_mx(b)
                sp.dma_start(dst.rearrange("o m -> m o"), mx[:]).then_inc(mx_out, 16)
                sp.wait_ge(mx_out, 16 * nb + 16)
                sp.dma_start(mmb[:], one_mx(b).to_broadcast([P, 16])).then_inc(mx_in, 16)
                for r in range(2):
                    sp.wait_ge(row_done, 2 * nb + r + 1)
                    sp.dma_start(one(rows_d, b)[:, r * HALF:(r + 1) * HALF],
                                 rowb[r].rearrange("p k i -> p (k i)")).then_inc(rows_out, 16)
                sp.wait_ge(rows_out, 32 * nb + 32)

            def one_mx(b):
                return mx_d[b:b + 1] if isinstance(b, int) else mx_d[bass.ds(b, 1)]

            def load_res(b, half, n):
                for g in range(2):
                    wait(sp, y_out, 16 * n)
                    sp.dma_start(xr[:, 4 * g:4 * g + 4, :], nodes(x, b, 2 * half + g)).then_inc(xr_in, 16)

            def store_res(b, half, n):
                sp.wait_ge(y_done, n + 1)
                for g in range(2):
                    sp.dma_start(nodes(out, b, 2 * half + g), xr[:, 4 * g:4 * g + 4, :]).then_inc(y_out, 16)

            for kb in range(KB):
                sp.dma_start(We[:, kb, :, 0:HO], w[:, kb * P:(kb + 1) * P, :].rearrange("h p e -> p h e")
                             ).then_inc(const_in, 16)
            sp.dma_start(aa[0:H, :], a_src[:, 0, :]).then_inc(const_in, 16)
            sp.dma_start(aa[H:2 * H, :], a_dst[:, 0, :]).then_inc(const_in, 16)
            for dst, src in ((gammaB[:], gamma), (betaB[:], beta), (biasB[:].rearrange("p h e -> p (h e)"), bias)):
                sp.dma_start(dst, src.rearrange("(o h) e -> o (h e)", o=1).to_broadcast([P, D])).then_inc(const_in, 16)
            load_x(0, 0, 0)
            for j in range(1, Q):
                load_x(0, j, start_x(j - 1) + 2)
            bounds_and_rows(0, 0)
            load_scores(0, 0, 0)
            load_scores(0, 1, 1)

            def batch(b, par, first, last):
                for k in range(UNITS):
                    n = UNITS * b + k
                    if k == 0 and not first:
                        store_res(b - 1, 0, 2 * b - 2)
                        load_res(b - 1, 1, 4 * b - 2)
                    if k == 3 and not first:
                        store_res(b - 1, 1, 2 * b - 1)
                    if k == 4:
                        load_res(b, 0, 4 * b)
                    if not last and k in (0, 2, 3):
                        for j in {0: (0,), 2: (1, 2), 3: (3,)}[k]:
                            load_x(b + 1, j, tp_at(b, f"x{j - 1}") + 2 if j else (start_x(3) + 2 if first else tp_at(b - 1, "x3") + 2))
                    if not last and k == 4:
                        bounds_and_rows(b + 1, b + 1)
                    if k + 2 < UNITS:
                        load_scores(b, k + 2, n + 2)
                    elif not last:
                        load_scores(b + 1, k + 2 - UNITS, n + 2)

            loop_batches(sp, None, 0, batch)
            store_res(NB - 1, 0, 2 * NB - 2)
            load_res(NB - 1, 1, 4 * NB - 2)
            store_res(NB - 1, 1, 2 * NB - 1)
            sp.wait_ge(y_out, 16 * 4 * NB)

        @block.gpsimd
        def _(pool):
            ps = Steps(p_step)

            def load_adj(b, m, taken):
                for i in range(2):
                    wait(pool, tp_free, taken - 1 + i)
                    pool.dma_start(stage[i][:], row_chunk(b, m, i)).then_inc(adj_in[i], 16)

            def prep_operands(b, par, h, branches=(0, 1)):
                if 0 in branches:
                    pool.wait_ge(bx_done, b + 1)
                    pool.wait_ge(rows_out, 32 * b + 32)
                    wait(pool, acc_full, 4 * (UNITS * b + h - 3))
                    pool.wait_ge(hs_done, b + 1)
                    settled(pool)
                    ps.chain(pool, nc.gpsimd.tensor_scalar(hs[:, h, :], hsN[:, h, :], 1.0, 0.0, ALU.mult, ALU.add))
                G8 = TILES // 2
                for j in branches:
                    for g in range(2):
                        t0 = g * G8
                        ps.chain(pool, nc.gpsimd.tensor_tensor(
                            Tt[:], hx[par][:, t0:t0 + G8, h, 0:E1],
                            Bx[:, j, h, t0:t0 + G8].unsqueeze(2).to_broadcast([P, G8, E1]), ALU.mult))
                        settled(pool)
                        hi = Xh[h][:, t0:t0 + G8, 2 * E1 * j:2 * E1 * j + E1]
                        ps.chain(pool, nc.gpsimd.tensor_scalar(hi, Tt[:], 1.0, 0.0, ALU.mult, ALU.add))
                        last = nc.gpsimd.tensor_tensor(Xh[h][:, t0:t0 + G8, 2 * E1 * j + E1:2 * E1 * (j + 1)],
                                                       Tt[:], hi, ALU.subtract)
                        if (j, g) != (1, 1):
                            ps.chain(pool, last)
                if 1 in branches:
                    last.then_inc(x_prep, 1)
                    pool.wait_ge(x_prep, H * b + h + 1)

            def combine(b, par, n, k, g):
                half, h = k // H, k % H
                t0 = half * HT + 4 * g
                if (k, g) == (0, 0):
                    pool.wait_ge(exp_done, 3 * b + 3)
                pool.wait_ge(acc_free, 4 * n + 2 * g + 2)
                a = accS[g][:].rearrange("p t (j s e) -> p t j s e", j=2, s=2)
                hi, lower = a[:, :, :, 0, :], a[:, :, 1, 0, :]
                ps.chain(pool, nc.gpsimd.tensor_tensor(hi, hi, a[:, :, :, 1, :], ALU.add))
                ps.chain(pool, nc.gpsimd.tensor_tensor(
                    lower, lower, rowf[par][:, h, t0:t0 + 4].unsqueeze(2).to_broadcast([P, 4, E1]), ALU.mult))
                nc.gpsimd.tensor_tensor(a[:, :, 0, 0, :], a[:, :, 0, 0, :], lower, ALU.add).then_inc(fin1, 1)
                pool.wait_ge(fin1, 2 * n + g + 1)

            def bc(t):
                return t[:].unsqueeze(1).to_broadcast([P, HT, D])

            def residual_in(n):
                pool.wait_ge(xr_in, 32 * n + 32)
                ps.chain(pool, nc.gpsimd.tensor_tensor(xr[:], xr[:], bc(betaB), ALU.add))

            def residual(par, half, n):
                v = hx[par][:, half * HT:(half + 1) * HT, :, 0:HO]
                g = gammaB[:].rearrange("p (h e) -> p h e", h=H).unsqueeze(1).to_broadcast([P, HT, H, HO])
                pool.wait_ge(ln1, n + 1)
                ps.chain(pool, nc.gpsimd.tensor_tensor(v, v, g, ALU.mult))
                y = xr[:].rearrange("p t (h e) -> p t h e", h=H)
                nc.gpsimd.tensor_tensor(y, y, v, ALU.add).then_inc(res, 1)
                pool.wait_ge(res, n + 1)

            ps.chain(pool, nc.gpsimd.memset(ident[:], 0.0))
            load_adj(0, 0, 0)
            nc.gpsimd.affine_select(out=ident[:], in_=ident[:], compare_op=ALU.not_equal, fill=1.0,
                                    base=0, pattern=[[-1, P]], channel_multiplier=1).then_inc(made, 1)
            for m in range(1, 5):
                load_adj(0, m, start_m(m - 1) + 2)
            pool.wait_ge(const_in, 16 * 7)
            prep_operands(0, 0, 0)
            prep_operands(0, 0, 1)
            load_adj(0, 5, start_m(4) + 2)
            prep_operands(0, 0, 2, (0,))

            def batch(b, par, first, last):
                for k in range(UNITS):
                    n = UNITS * b + k
                    if k == 0 and not first:
                        load_adj(b, 5, tp_at(b - 1, "m12") + 2)
                    elif k == 1:
                        load_adj(b, 6, tp_at(b, "m5") + 2)
                    elif k > 2 and not last:
                        load_adj(b + 1, k - 3, tp_at(b, f"m{k + 4}") + 2)
                    before = {0: (b, par, 2, (1,)), 1: (b, par, 3, (1,))}.get(k)
                    after = {0: [(b, par, 3, (0,))]}.get(k, [])
                    if k in (6, 7) and not last:
                        before = (b + 1, 1 - par, k - 6, (1 if k == 6 else 0,))
                    if k == 5 and not last:
                        after = [(b + 1, 1 - par, 0, (0,))]
                    if k == 7 and not last:
                        after = [(b + 1, 1 - par, 1, (1,)), (b + 1, 1 - par, 2, (0,))]
                    if k == 0 and not first:
                        combine(b - 1, 1 - par, n - 1, UNITS - 1, 1)
                    elif k > 0:
                        combine(b, par, n - 1, k - 1, 1)
                    if before:
                        prep_operands(*before)
                    combine(b, par, n, k, 0)
                    if k == 1 and not first:
                        residual_in(2 * b - 1)
                    if k == 1:
                        load_adj(b, 7, tp_at(b, "m6") + 2)
                    if k == 1 and not first:
                        residual(1 - par, 1, 2 * b - 1)
                    if k == 4:
                        residual_in(2 * b)
                    if k == 6:
                        residual(par, 0, 2 * b)
                    for operands in after:
                        prep_operands(*operands)

            loop_batches(pool, ps, POOL_STEPS, batch)
            combine(NB - 1, (NB - 1) % 2, UNITS * NB - 1, UNITS - 1, 1)
            residual_in(2 * NB - 1)
            residual((NB - 1) % 2, 1, 2 * NB - 1)

        @block.scalar
        def _(act):
            def compare(b, k, n, q):
                h = k % H
                if q == 0:
                    act.wait_ge(d_done, b + 1)
                    act.wait_ge(sB_in[k % 2], n_half(b, k) * 16 + 16)
                wait(act, gl_done, 4 * n + q - 1)
                settled(act)
                for c in range(3 if q in DVE_QUARTERS else 4):
                    last = nc.scalar.activation(Us[q % 2][:, :, c], sB[k % 2][:], ACT.Relu,
                                                bias=dpos[:, h, 4 * q + c:4 * q + c + 1], scale=BIG, saturate=False)
                last.then_inc(u_done, 1)

            def n_half(b, k):
                return (UNITS // 2) * b + k // 2

            def take(n, p):
                act.wait_ge(acc_full, 4 * n + p + 1)
                if p % 2 == 0:
                    wait(act, fin2, 2 * n + p // 2 - 1)
                b0 = 2 * p % 4
                nc.scalar.copy(accS[p // 2][:, b0:b0 + 2, :], acc[:, b0:b0 + 2, 0:4 * E1]).then_inc(acc_free, 1)

            def take_h(b, par, t):
                v = TILES * b + t
                if t % (TILES // 2) == 0:
                    wait(act, res, 2 * b - (3 if t == 0 else 2))
                act.wait_ge(h_full, v + 1)
                nc.scalar.copy(hx[par][:, t, :, :].rearrange("p h e -> p (h e)"), hp[:, t % 2, 0:WE]).then_inc(h_out, 1)

            def factors(b, par):
                act.wait_ge(dd_done, b + 1)
                wait(act, x_prep, 4 * b)
                wait(act, fin1, 2 * UNITS * (b - 1))
                for dst, src, scale in ((Bx[:, 0], dd, 1.0), (Bx[:, 1], dd, SLOPE), (rowf[par][:], sm, SLOPE - 1.0)):
                    nc.scalar.activation(dst, src[:], ACT.Exp, scale=scale).then_inc(exp_done, 1)

            def deviation(n, src, dst, src_sem, dst_sem):
                act.wait_ge(src_sem, n + 1)
                nc.scalar.activation(dst, src, ACT.Sqrt).then_inc(dst_sem, 1)

            for t in range(TILES):
                take_h(0, 0, t)
            factors(0, 0)
            for q in range(4):
                compare(0, 0, 0, q)

            def stat(which):
                return (vv[:], rs2[:], var2, std2) if which else (lnA[:, 3, :], rs1[:], var1, std1)

            def batch(b, par, first, last):
                for k in range(UNITS):
                    n = UNITS * b + k
                    for q in range(5):
                        if q < 4 and k + 1 < UNITS:
                            compare(b, k + 1, n + 1, q)
                        elif q < 4 and not last:
                            compare(b + 1, 0, n + 1, q)
                        if q > 0:
                            take(n, q - 1)
                        projected = {(2, 1): 0, (2, 3): 1, (3, 1): 2, (4, 1): 3}.get((k, q))
                        if projected is not None and not last:
                            for c in range(4):
                                take_h(b + 1, 1 - par, 4 * projected + c)
                        if q == 2 and not last and k == 5:
                            factors(b + 1, 1 - par)
                    if k in (0, 2) and not first:
                        deviation(2 * b - 1, *stat(k))
                    if k in (4, 7):
                        deviation(2 * b, *stat(k - 4))

            loop_batches(act, None, 0, batch)
            deviation(2 * NB - 1, *stat(0))
            deviation(2 * NB - 1, *stat(1))

        @block.tensor
        def _(pe):
            def tp_bank(u):
                wait(pe, tp_free, u - 1)

            def turn_x(b, j, u):
                pe.wait_ge(x_in, 16 * (Q * b + j) + 16)
                for kb in range(KB):
                    tp_bank(u + kb)
                    for c in range(4):
                        last = nc.tensor.transpose(tp[:, kb, c * P:(c + 1) * P], xs[:, c, kb * P:(kb + 1) * P], ident[:])
                    last.then_inc(tp_full, 1)

            def project(b, j, u):
                pe.wait_ge(tp_free, u + 2)
                for c in range(4):
                    v = TILES * b + 4 * j + c
                    wait(pe, h_out, v - 1)
                    for kb in range(KB):
                        last = nc.tensor.matmul(hp[:, c % 2, 0:WE], xT[:, kb, c * P:(c + 1) * P],
                                                We[:, kb, :, :].rearrange("p h e -> p (h e)"),
                                                start=(kb == 0), stop=(kb == KB - 1))
                    last.then_inc(h_full, 1)

            def turn_scores(b, u):
                pe.wait_ge(pm_done, b + 1)
                tp_bank(u)
                nc.tensor.transpose(tp[0:16, 0, 0:P], pm[:], ident[:]).then_inc(tp_full, 1)
                pe.wait_ge(sd_done, b + 1)
                for r in range(4):
                    tp_bank(u + 1 + r)
                    for c in range(4):
                        last = nc.tensor.transpose(tp[0:8, (1 + r) % 2, c * P:(c + 1) * P],
                                                   sd[:, 4 * r + c, :, :].rearrange("p h s -> p (h s)"), ident[:])
                    last.then_inc(tp_full, 1)
                pe.wait_ge(xtot_done, b + 1)
                tp_bank(u + 5)
                for kb in range(KB):
                    last = nc.tensor.matmul(tp[:, 1, 0:WE], xtot[:, kb:kb + 1].to_broadcast([P, P]),
                                            We[:, kb, :, :].rearrange("p h e -> p (h e)"),
                                            start=(kb == 0), stop=(kb == KB - 1))
                last.then_inc(tp_full, 1)

            def turn_adj(b, m, u):
                for i in range(2):
                    pe.wait_ge(adj_in[i], 16 * (8 * b + m) + 16)
                    tp_bank(u + i)
                    for q in range(Q):
                        last = nc.tensor.transpose(tp[:, i, q * P:(q + 1) * P],
                                                   stage[i][:, 512 * q:512 * q + 512].bitcast(F32), ident[:])
                    last.then_inc(tp_full, 1)

            def sums(n, k, t):
                h, buf, bank = k % H, k % 2, t % 4
                for q in range(Q):
                    for c in range(4):
                        first = q == 0 and c == 0
                        nc.tensor.matmul(acc[:, bank, 0:2 * E1], Gm[buf][:, q, t * P:(t + 1) * P, c],
                                         Xh[h][:, 4 * q + c, 0:2 * E1], start=first, stop=False, skip_group_check=True)
                        last = nc.tensor.matmul(acc[:, bank, 2 * E1:4 * E1], Lm[buf][:, q, t * P:(t + 1) * P, c],
                                                Xh[h][:, 4 * q + c, 2 * E1:4 * E1], start=False,
                                                stop=(q == Q - 1 and c == 3), skip_group_check=True)
                        if first:
                            nc.tensor.matmul(acc[:, bank, 0:E1], ones[:], hs[:, h, :], start=False, stop=False,
                                             skip_group_check=True)
                return last

            pe.wait_ge(made, 1)
            pe.wait_ge(const_in, 16 * 7)
            for kb in range(KB):
                for h in range(H):
                    last = nc.tensor.transpose(tp[0:HO, kb, h * P:(h + 1) * P], We[:, kb, h, 0:HO], ident[:])
                last.then_inc(tp_full, 1)
            tp_bank(2)
            nc.tensor.transpose(tp[0:HO, 0, 0:8], aa[:], ident[0:8, 0:8]).then_inc(tp_full, 1)
            pe.wait_ge(tp_free, 3)
            tp_bank(3)
            for kb in range(KB):
                for h in range(H):
                    last = nc.tensor.matmul(tp[:, 1, 2 * (H * kb + h):2 * (H * kb + h) + 2], xT[0:HO, kb, h * P:(h + 1) * P],
                                            aT[:, h:h + H + 1:H], start=True, stop=True)
            last.then_inc(tp_full, 1)
            pe.wait_ge(tp_free, 4)
            for j in range(Q):
                turn_x(0, j, start_x(j))
                project(0, j, start_x(j))
                turn_adj(0, j, start_m(j))
            turn_scores(0, TP_PM0)
            pe.wait_ge(dset, 1)
            turn_adj(0, 4, start_m(4))

            def batch(b, par, first, last):
                for k in range(UNITS):
                    n = UNITS * b + k

                    def beside(p):
                        chunk = k + 5
                        if chunk < 8 and p == (0 if k == 2 else 2):
                            turn_adj(b, chunk, tp_at(b, f"m{chunk}", last))
                        if not last:
                            turned = {(1, 3): 0, (2, 1): 1, (2, 3): 2, (3, 2): 3}.get((k, p))
                            projected = {(2, 0): 0, (2, 2): 1, (3, 0): 2, (4, 0): 3}.get((k, p))
                            if turned is not None:
                                turn_x(b + 1, turned, tp_at(b, f"x{turned}"))
                            if projected is not None:
                                project(b + 1, projected, tp_at(b, f"x{projected}"))
                        if k == 4 and p == 3 and not last:
                            turn_scores(b + 1, tp_at(b, "pm"))
                        if chunk >= 8 and p == (3 if k in (3, 4) else 2) and not last:
                            turn_adj(b + 1, chunk - 8, tp_at(b, f"m{chunk}"))


                    pe.wait_ge(gl_done, 4 * n + 4)
                    if k < H:
                        pe.wait_ge(x_prep, 4 * b + k + 1)
                    for p in range(HT // 2):
                        wait(pe, acc_free, 4 * n + p - 1)
                        settled(pe)
                        sums(n, k, 2 * p)
                        sums(n, k, 2 * p + 1).then_inc(acc_full, 1)
                        beside(p)

            loop_batches(pe, None, 0, batch)
            pe.wait_ge(flag_in, 1)
            nc.tensor.matmul(tp[0:1, 0, 0:1], guard[:, 0:1], guard[:, 1:2], start=True, stop=True).then_inc(flag_sum, 1)

        @block.vector
        def _(dve):
            vs = Steps(v_step)
            V = nc.vector

            def chain(ins):
                vs.chain(dve, ins)

            def n_half(b, k):
                return (UNITS // 2) * b + k // 2

            def take_x(b, j, u):
                wait(dve, h_full, TILES * b + 4 * j)
                if j == 0:
                    wait(dve, x_prep, H * b)
                for kb in range(KB):
                    dve.wait_ge(tp_full, u + kb + 1)
                    V.tensor_scalar(xT[:, kb, :], tp[:, kb, :], 1.0, None, ALU.mult, ALU.add,
                                    accum_out=xsum[:, kb, j:j + 1]).then_inc(tp_free, 1)

            def scores(b, par):
                dve.wait_ge(h_out, TILES * b + TILES)
                chain(V.tensor_scalar(sd[:], hx[par][:, :, :, HO:EX], QUANTUM, QUANTUM, ALU.add, ALU.subtract))
                V.tensor_scalar(hx[par][:, :, :, HO:E1], hx[par][:, :, :, HO:E1], 0.0, 1.0, ALU.mult, ALU.add
                                ).then_inc(sd_done, 1)
                view = sd[:].rearrange("p t h s -> p (h s) t")
                V.tensor_reduce(pm[:, 0:8], view, AX.X, ALU.max)
                V.tensor_reduce(pm[:, 8:16], view, AX.X, ALU.min, negate=True).then_inc(pm_done, 1)
                V.tensor_reduce(xtot[:], xsum[:], AX.X, ALU.add).then_inc(xtot_done, 1)

            def feature_guard(par):
                chain(V.tensor_reduce(guard[:, 2:3], hx[par][:, :, :, 0:HO], AX.XYZ, ALU.max, apply_absolute_value=True))
                chain(V.tensor_tensor(viol[:, 3:4], viol[:, 3:4], guard[:, 2:3], ALU.max))

            def bounds(u):
                dve.wait_ge(tp_full, u + 1)
                V.tensor_reduce(mx[:], tp[0:16, 0, 0:P], AX.X, ALU.max).then_inc(tp_free, 1)
                dve.wait_ge(tp_free, u + 1)
                dve.sem_inc(mx_done, 1)

            def rows(b, u):
                wait(dve, h_full, TILES * b + TILES)
                for r in range(4):
                    dve.wait_ge(tp_full, u + 2 + r)
                    V.tensor_copy(rowb[r // 2][:, r % 2, :], tp[0:8, (1 + r) % 2, :]).then_inc(tp_free, 1)
                    if r % 2:
                        dve.wait_ge(tp_free, u + 2 + r)
                        dve.sem_inc(row_done, 1)

            def mean_parts(b, u):
                dve.wait_ge(tp_full, u + 6)
                V.tensor_scalar(hf[:, :, 0:HO], tp[:, 1, 0:WE].rearrange("p (h e) -> p h e", h=H)[:, :, 0:HO], TINY,
                                None, ALU.mult).then_inc(tp_free, 1)
                dve.wait_ge(tp_free, u + 6)
                chain(V.memset(hf[:, :, HO:E1], N * TINY))
                chain(V.tensor_copy(hpart[:, 0], hf[:]))
                chain(V.tensor_tensor(hf[:], hf[:], hpart[:, 0], ALU.subtract))
                chain(V.tensor_copy(hpart[:, 1], hf[:]))
                chain(V.tensor_tensor(hpart[:, 2], hf[:], hpart[:, 1], ALU.subtract))
                wait(dve, x_prep, H * b)
                chain(V.tensor_scalar(hsN[:], hpart[:, 0], ident[:, 0:1], None, ALU.mult))
                chain(V.scalar_tensor_tensor(hsN[:], hpart[:, 1], ident[:, 1:2], hsN[:], ALU.mult, ALU.add))
                V.scalar_tensor_tensor(hsN[:], hpart[:, 2], ident[:, 2:3], hsN[:], ALU.mult, ALU.add
                                       ).then_inc(hs_done, 1)

            def factors_in(b):
                dve.wait_ge(mx_in, 16 * b + 16)
                wait(dve, exp_done, 3 * b)
                dve.wait_ge(sd_done, b + 1)
                sv = sd[:].rearrange("p t h s -> p s h t")
                bc = mmb[:, 1:8:2].unsqueeze(2).to_broadcast([P, H, TILES])
                V.tensor_tensor(dd[:], sv[:, 1], bc, ALU.subtract)
                V.tensor_tensor(sm[:], sv[:, 0], bc, ALU.add).then_inc(dd_done, 1)
                V.tensor_tensor(guard[:, 4:8], mmb[:, 1:8:2], mmb[:, 9:16:2], ALU.add)
                chain(V.tensor_tensor(guard[:, 8:12], mmb[:, 8:16:2], mmb[:, 1:8:2], ALU.subtract))
                V.tensor_reduce(guard[:, 12:13], guard[:, 4:8], AX.X, ALU.max)
                V.tensor_reduce(guard[:, 13:14], guard[:, 8:12], AX.X, ALU.max)
                chain(V.tensor_reduce(guard[:, 14:15], mmb[:], AX.X, ALU.max))
                chain(V.tensor_tensor(viol[:, 0:3], viol[:, 0:3], guard[:, 12:15], ALU.max))

            def factors_out(b):
                dve.wait_ge(exp_done, 3 * b + 2)
                V.tensor_scalar(Bx[:], Bx[:], SCALE, None, ALU.mult).then_inc(bx_done, 1)

            def operands_d(b):
                wait(dve, u_done, 4 * UNITS * b)
                wait(dve, gl_done, 4 * UNITS * b)
                sv = sd[:].rearrange("p t h s -> p s h t")
                V.tensor_scalar(dpos[:], sv[:, 1], BIG, None, ALU.mult)
                V.tensor_scalar(dneg[:], sv[:, 1], -1.0, None, ALU.mult).then_inc(d_done, 1)

            def take_adj(b, m, u, n_gl):
                half = m // 4
                wait(dve, gl_done, n_gl)
                for i in range(2):
                    dve.wait_ge(adj_in[i], 16 * (8 * b + m) + 16)
                    wait(dve, tp_free, u + i)
                    V.tensor_tensor(seen[:], seen[:], stage[i][:].bitcast(U32), ALU.bitwise_or)
                    at = (2 * (m % 4) + i) * P
                    dve.wait_ge(tp_full, u + i + 1)
                    V.tensor_scalar(Mt[half][:, :, at:at + P], tp[:, i, :].rearrange("p (q i) -> p q i", q=Q).bitcast(U32),
                                    5, EDGE4, ALU.logical_shift_left, ALU.bitwise_and).then_inc(tp_free, 1)

            def compare(b, k, n, q):
                if q not in DVE_QUARTERS:
                    return
                dve.wait_ge(sB_in[k % 2], n_half(b, k) * 16 + 16)
                dve.wait_ge(d_done, b + 1)
                wait(dve, gl_done, 4 * n + q - 1)
                settled(dve)
                V.tensor_scalar(Us[q % 2][:, :, 3], sB[k % 2][:], dneg[:, k % H, 4 * q + 3:4 * q + 4], None,
                                ALU.is_gt, saturate=False).then_inc(v_cmp, 1)

            def masks(k, n, q, tp_done):
                half, buf = k // H, k % 2
                if q == 0:
                    wait(dve, acc_full, 4 * (n - 1))
                    wait(dve, tp_free, tp_done)
                if q in DVE_QUARTERS:
                    dve.wait_ge(v_cmp, len(DVE_QUARTERS) * n + DVE_QUARTERS.index(q) + 1)
                dve.wait_ge(u_done, 4 * n + q + 1)
                u = Us[q % 2][:].rearrange("p i c -> p (i c)").bitcast(U32)
                V.tensor_tensor(words(Gm[buf])[:, q], u, Mt[half][:, q], ALU.bitwise_and)
                V.scalar_tensor_tensor(words(Lm[buf])[:, q], u, 0xFFFFFFFF, Mt[half][:, q], ALU.bitwise_xor,
                                       ALU.bitwise_and).then_inc(gl_done, 1)

            def finish(par, n, k, g):
                half, h = k // H, k % H
                dve.wait_ge(fin1, 2 * n + g + 1)
                chain(V.reciprocal(rdn[:, g, :], accS[g][:, :, HO]))
                num = accS[g][:, :, 0:HO]
                chain(V.tensor_tensor(num, num, rdn[:, g, :].unsqueeze(2).to_broadcast([P, 4, HO]), ALU.mult))
                chain(V.tensor_tensor(num, num, biasB[:, h, :].unsqueeze(1).to_broadcast([P, 4, HO]), ALU.add))
                dst = hx[par][:, half * HT + 4 * g:half * HT + 4 * g + 4, h, 0:HO]
                V.scalar_tensor_tensor(dst, num, 0.0, dst, ALU.max, ALU.add).then_inc(fin2, 1)

            def head_stats(par, half, n):
                dve.wait_ge(fin2, 8 * n + 8)
                wait(dve, std1, n)
                wait(dve, ln1, n)
                for i in range(HT * H):
                    last = V.bn_stats(st[:, i, :], hx[par][:, half * HT + i // H, i % H, 0:HO])
                chain(last)
                V.tensor_tensor(lnA[:, 1, :], st[:, :, 1], st[:, :, 4], ALU.subtract)
                V.tensor_tensor(lnA[:, 2, :], st[:, :, 2], st[:, :, 5], ALU.add)
                chain(V.tensor_tensor(lnA[:, 0, :], st[:, :, 1], st[:, :, 4], ALU.add))
                V.tensor_scalar(lnA[:, 4, :], lnA[:, 0, :], 0.5, None, ALU.mult)
                chain(V.tensor_tensor(lnA[:, 1, :], lnA[:, 1, :], lnA[:, 1, :], ALU.mult))
                chain(V.scalar_tensor_tensor(lnA[:, 2, :], lnA[:, 1, :], HO / 4.0, lnA[:, 2, :], ALU.mult, ALU.add))
                V.tensor_scalar(lnA[:, 3, :], lnA[:, 2, :], 1.0 / HO, EPS_HEAD, ALU.mult, ALU.add).then_inc(var1, 1)

            def head_apply(par, half, n):
                v = hx[par][:, half * HT:(half + 1) * HT, :, 0:HO]
                bc = lambda t: t.rearrange("p (t h) -> p t h", h=H).unsqueeze(3).to_broadcast([P, HT, H, HO])
                dve.wait_ge(var1, n + 1)
                chain(V.tensor_tensor(v, v, bc(lnA[:, 4, :]), ALU.subtract))
                dve.wait_ge(std1, n + 1)
                chain(V.reciprocal(rs1[:], rs1[:]))
                V.tensor_tensor(v, v, bc(rs1[:]), ALU.mult).then_inc(ln1, 1)

            def out_stats(n):
                dve.wait_ge(res, n + 1)
                wait(dve, std2, n)
                wait(dve, y_done, n)
                for t in range(HT):
                    last = V.bn_stats(st2[:, t, :], xr[:, t, :])
                chain(last)
                settled(dve)
                for t in range(HT):
                    last = V.bn_aggr(mv[:, t, :], st2[:, t, :])
                chain(last)
                V.tensor_scalar(vv[:], mv[:, :, 1], EPS_OUT, None, ALU.add).then_inc(var2, 1)

            def out_apply(n):
                dve.wait_ge(std2, n + 1)
                chain(V.reciprocal(rs2[:], rs2[:]))
                for t in range(HT):
                    last = V.tensor_scalar(xr[:, t, :], xr[:, t, :], mv[:, t, 0:1], rs2[:, t:t + 1], ALU.subtract, ALU.mult)
                last.then_inc(y_done, 1)

            V.memset(ones[:], 1.0)
            V.memset(seen[:], 0)
            V.memset(viol[:], 0.0)
            V.memset(guard[:], 1.0).then_inc(dset, 1)
            dve.wait_ge(dset, 1)
            dve.wait_ge(made, 1)
            for kb in range(KB):
                dve.wait_ge(tp_full, kb + 1)
                V.tensor_copy(xT[0:HO, kb, :], tp[0:HO, kb, :]).then_inc(tp_free, 1)
            dve.wait_ge(tp_full, 3)
            V.tensor_copy(aT[:], tp[0:HO, 0, 0:8]).then_inc(tp_free, 1)
            dve.wait_ge(tp_full, 4)
            V.tensor_copy(We[:, :, :, HO:EX], tp[:, 1, 0:4 * H].rearrange("p (k h s) -> p k h s", k=KB, h=H)
                          ).then_inc(tp_free, 1)
            for j in range(Q):
                take_x(0, j, start_x(j))
                take_adj(0, j, start_m(j), 0)
            scores(0, 0)
            bounds(TP_PM0)
            rows(0, TP_PM0)
            mean_parts(0, TP_PM0)
            operands_d(0)
            factors_in(0)
            factors_out(0)
            for q in range(4):
                compare(0, 0, 0, q)
                masks(0, 0, q, start_m(3) + 2)
            take_adj(0, 4, start_m(4), 0)
            feature_guard(0)

            def batch(b, par, first, last):
                for k in range(UNITS):
                    n = UNITS * b + k
                    ahead = (b, k + 1) if k + 1 < UNITS else (b + 1, 0)
                    make = k + 1 < UNITS or not last
                    tp_done = tp_at(b, "m7", last) + 2 if ahead[1] == H else tp_at(b, "m11") + 2 if ahead[1] == 0 else 0

                    def cmp_(q):
                        if make:
                            compare(*ahead, n + 1, q)

                    def msk_(q):
                        if make:
                            masks(ahead[1], n + 1, q, tp_done)

                    def adj_():
                        chunk = k + 5
                        if chunk < 8:
                            take_adj(b, chunk, tp_at(b, f"m{chunk}", last), 4 * UNITS * b)
                        elif not last:
                            n_gl = 4 * UNITS * b + (4 * H if chunk < 12 else 4 * UNITS)
                            take_adj(b + 1, chunk - 8, tp_at(b, f"m{chunk}"), n_gl)

                    if k == 7 and not last:
                        operands_d(b + 1)
                    cmp_(0)
                    cmp_(1)
                    if k == 5 and not last:
                        factors_in(b + 1)
                    msk_(0)
                    if k > 0:
                        finish(par, n - 1, k - 1, 0)
                    elif not first:
                        finish(1 - par, n - 1, UNITS - 1, 0)
                    cmp_(2)
                    if k == 2:
                        adj_()
                    if k == 3 and not first:
                        out_apply(2 * b - 1)
                    if k == 0 and not first:
                        out_apply(2 * b - 2)
                    msk_(1)
                    cmp_(3)
                    if k > 0:
                        finish(par, n - 1, k - 1, 1)
                    elif not first:
                        finish(1 - par, n - 1, UNITS - 1, 1)
                    if k == 2 and not last:
                        take_x(b + 1, 1, tp_at(b, "x1"))
                    if k == 4 and not last:
                        scores(b + 1, 1 - par)
                    if k == 0 and not first:
                        head_stats(1 - par, 1, 2 * b - 1)
                    if k == 1 and not first:
                        head_apply(1 - par, 1, 2 * b - 1)
                    if k == 2 and not first:
                        out_stats(2 * b - 1)
                    msk_(2)
                    if k == 4:
                        head_stats(par, 0, 2 * b)
                    if k == 5:
                        head_apply(par, 0, 2 * b)
                    if k == 6 and not last:
                        feature_guard(1 - par)
                    if k == 7:
                        out_stats(2 * b)
                    if k == 5 and not last:
                        factors_out(b + 1)
                    if k not in (2, 3, 4):
                        adj_()
                    msk_(3)
                    if k in (1, 2, 3) and not last:
                        j = {1: 0, 2: 2, 3: 3}[k]
                        take_x(b + 1, j, tp_at(b, f"x{j}"))
                    if k == 4 and not last:
                        u = tp_at(b, "pm")
                        bounds(u)
                        rows(b + 1, u)
                        mean_parts(b + 1, u)
                    if k in (3, 4):
                        adj_()

            loop_batches(dve, vs, DVE_STEPS, batch)
            par = (NB - 1) % 2
            finish(par, UNITS * NB - 1, UNITS - 1, 0)
            finish(par, UNITS * NB - 1, UNITS - 1, 1)
            out_apply(2 * NB - 2)
            head_stats(par, 1, 2 * NB - 1)
            head_apply(par, 1, 2 * NB - 1)
            out_stats(2 * NB - 1)
            out_apply(2 * NB - 1)

            chain(V.tensor_scalar(seen[:], seen[:], NOT_ONE4, None, ALU.bitwise_and))
            chain(V.tensor_reduce(guard[:, 3:4], seen[:], AX.X, ALU.max))
            chain(V.tensor_scalar(guard[:, 3:4], guard[:, 3:4], 0.0, None, ALU.is_gt))
            for i, limit in enumerate((SPAN_LIMIT, LOW_LIMIT, SIZE_LIMIT, H_LIMIT)):
                last = V.tensor_scalar(viol[:, i:i + 1], viol[:, i:i + 1], limit, None, ALU.is_gt)
            chain(last)
            chain(V.tensor_reduce(guard[:, 0:1], viol[:], AX.X, ALU.max))
            V.tensor_tensor(guard[:, 0:1], guard[:, 0:1], guard[:, 3:4], ALU.max).then_inc(flag_in, 1)
            dve.wait_ge(flag_sum, 1)
            V.tensor_copy(flag[:], tp[0:1, 0, 0:1]).then_inc(flag_set, 1)

def general_pass(nc, flag, x, adj, w, a_src, a_dst, bias, gamma, beta, out):
    NB, N, D = x.shape
    H, _, HO = w.shape
    TY = a_src.shape[1]
    KB = D // P
    TILES = N // P
    ES = 2 * TY
    SC = H * ES

    ctx = ExitStack()
    with ctx:
        def sb(name, shape, dt=F32):
            return ctx.enter_context(nc.sbuf_tensor("g_" + name, shape, dt))

        def psum(name, shape):
            return ctx.enter_context(nc.psum_tensor("g_" + name, shape, F32))

        def sem(name):
            return ctx.enter_context(nc.semaphore("g_" + name))

        hx = sb("hx", [P, TILES, H, HO])
        ho = sb("ho", [P, TILES, D])
        sc = sb("sc", [P, TILES, SC])
        rows = sb("rows", [SC, N])
        dB = sb("dB", [P, TY, N])
        adjI = sb("adjI", [P, N], I32)
        adjF = sb("adjF", [P, N])
        wt = sb("wt", [P, N])
        part = sb("part", [P, N])
        prob = sb("prob", [P, N])
        probT = sb("probT", [P, N])
        xin = sb("xin", [P, D])
        xT = sb("xT", [P, KB, P])
        Wf = sb("Wf", [P, KB, H, HO])
        Ws = sb("Ws", [P, KB, SC])
        wT = sb("wT", [HO, KB, H * P])
        aa = sb("aa", [SC, HO])
        aT = sb("aT", [HO, SC])
        ident = sb("ident", [P, P])
        gammaB = sb("gammaB", [P, D])
        betaB = sb("betaB", [P, D])
        biasB = sb("biasB", [P, D])
        mhalf = sb("mhalf", [P, 1])
        es = sb("es", [P, TY])
        nmax = sb("nmax", [P, 1])
        den = sb("den", [P, 1])
        o = sb("o", [P, HO])
        y = sb("y", [P, D])
        st = sb("st", [P, 6])
        mv = sb("mv", [P, 2])
        vv = sb("vv", [P, 1])
        rs = sb("rs", [P, 1])
        tr = psum("tr", [P, 4, 512])
        pr = psum("pr", [P, 2, 512])
        ao = psum("ao", [P, 512])
        rows_d = nc.dram_tensor("all_score_rows", [SC, N], F32).ap()

        const_in, x_in, adj_in, ed_in, xr_in = (sem(n) for n in ("const_in", "x_in", "adj_in", "ed_in", "xr_in"))
        rows_out, y_out = sem("rows_out"), sem("y_out")
        made = sem("made")
        w_turned = sem("w_turned")
        w_taken = sem("w_taken")
        we_full = sem("we_full")
        we_done = sem("we_done")
        x_turned = sem("x_turned")
        xT_done = sem("xT_done")
        h_full = sem("h_full")
        h_taken = sem("h_taken")
        adj_taken = sem("adj_taken")
        w_done = sem("w_done")
        p_done = sem("p_done")
        pt_full = sem("pt_full")
        pt_out = sem("pt_out")
        o_full = sem("o_full")
        var_done, rs_done = sem("var_done"), sem("rs_done")
        var2_done, rs2_done = sem("var2_done"), sem("rs2_done")
        y_done = sem("y_done")
        start_step, unit_step, out_step = sem("start_step"), sem("unit_step"), sem("out_step")
        rows_free = sem("rows_free")
        settled_at = sem("settled_at")

        def settled(eng):
            eng.sem_inc(settled_at, 1)

        def tile_of(t, b, r):
            return t.rearrange("b n d -> (b n) d")[bass.ds(b * N + r * P, P)]

        def units(eng, b, unit):
            for h in range(H):
                with eng.Fori(0, TILES) as r:
                    unit(b * (H * TILES) + (r + h * TILES), h, r)

        block = ctx.enter_context(nc.Block())

        @block.sync
        def _(sp):
            with sp.If(sp.value_load(flag[0:1, 0:1]) != 0):
                for kb in range(KB):
                    sp.dma_start(Wf[:, kb], w[:, kb * P:(kb + 1) * P, :].rearrange("h p e -> p h e")
                                 ).then_inc(const_in, 16)
                for h in range(H):
                    for s, a in enumerate((a_src, a_dst)):
                        at = h * ES + s * TY
                        sp.dma_start(aa[at:at + TY, :], a[h]).then_inc(const_in, 16)
                for dst, src in ((gammaB, gamma), (betaB, beta), (biasB, bias)):
                    sp.dma_start(dst[:], src.rearrange("(o h) e -> o (h e)", o=1).to_broadcast([P, D])
                                 ).then_inc(const_in, 16)
                sp.sem_inc(rows_free, 1)
                with sp.Fori(0, NB) as b:
                    with sp.Fori(0, TILES) as t:
                        v = b * TILES + t
                        sp.wait_ge(x_turned, v + 1)
                        settled(sp)
                        sp.dma_start(xin[:], tile_of(x, b, t)).then_inc(x_in, 16)
                    sp.wait_ge(h_taken, (b + 1) * TILES + 1)
                    sp.dma_start(rows_d, rows[:]).then_inc(rows_out, 16)
                    sp.wait_ge(rows_out, (b + 1) * 16)
                    sp.sem_inc(rows_free, 1)
                    for h in range(H):
                        sp.wait_ge(w_done, b * (H * TILES) + (h * TILES + 1))
                        src = rows_d[h * ES + TY:(h + 1) * ES].rearrange("(o t) n -> o (t n)", o=1)
                        sp.dma_start(dB[:].rearrange("p t n -> p (t n)"), src.to_broadcast([P, TY * N])).then_inc(ed_in, 16)
                        with sp.Fori(0, TILES) as r:
                            sp.wait_ge(adj_taken, b * (H * TILES) + (r + h * TILES) + 1)
                            settled(sp)
                            sp.dma_start(adjI[:], tile_of(adj, b, r)).then_inc(adj_in, 16)
                    with sp.Fori(0, TILES) as r:
                        v = b * TILES + r
                        sp.wait_ge(x_turned, (b + 1) * TILES + 1)
                        settled(sp)
                        sp.dma_start(xin[:], tile_of(x, b, r)).then_inc(xr_in, 16)
                        sp.wait_ge(y_done, v + 1)
                        settled(sp)
                        sp.dma_start(tile_of(out, b, r), y[:]).then_inc(y_out, 16)
                        sp.wait_ge(y_out, (v + 1) * 16)
                        settled(sp)
                sp.wait_ge(y_out, NB * TILES * 16)
            sp.nop()

        @block.gpsimd
        def _(pool):
            with pool.If(pool.value_load(flag[0:1, 0:1]) != 0):
                nc.gpsimd.memset(ident[:], 0.0)
                nc.gpsimd.memset(mhalf[:], -0.5).then_inc(start_step, 1)
                pool.wait_ge(start_step, 1)
                nc.gpsimd.affine_select(out=ident[:], in_=ident[:], compare_op=ALU.not_equal, fill=1.0,
                                        base=0, pattern=[[-1, P]], channel_multiplier=1).then_inc(made, 1)
                pool.wait_ge(made, 1)

                def rstd(index, src_sem, dst_sem):
                    pool.wait_ge(src_sem, index + 1)
                    nc.gpsimd.tensor_tensor(rs[:], vv[:], mhalf[:], ALU.pow).then_inc(dst_sem, 1)

                with pool.Fori(0, NB) as b:
                    units(pool, b, lambda u, h, r: rstd(u, var_done, rs_done))
                    with pool.Fori(0, TILES) as r:
                        rstd(b * TILES + r, var2_done, rs2_done)
            pool.nop()

        @block.scalar
        def _(act):
            with act.If(act.value_load(flag[0:1, 0:1]) != 0):
                def unit(u, h, r):
                    act.wait_ge(w_done, u + 2)
                    nc.scalar.activation(prob[:], wt[:], ACT.Exp, bias=nmax[:, 0:1], scale=1.0,
                                         accum_out=den[:, 0:1]).then_inc(p_done, 1)
                    act.wait_ge(pt_full, u + 1)
                    nc.scalar.copy(probT[:], tr[:].rearrange("p b i -> p (b i)")).then_inc(pt_out, 1)

                with act.Fori(0, NB) as b:
                    units(act, b, unit)
            act.nop()

        @block.tensor
        def _(pe):
            with pe.If(pe.value_load(flag[0:1, 0:1]) != 0):
                pe.sem_inc(x_turned, 1)
                pe.wait_ge(made, 1)
                pe.wait_ge(const_in, 16 * (KB + 2 * H + 3))
                for kb in range(KB):
                    for h in range(H):
                        nc.tensor.transpose(tr[0:HO, kb, h * P:(h + 1) * P], Wf[:, kb, h, :], ident[:])
                nc.tensor.transpose(tr[0:HO, KB, 0:SC], aa[:], ident[0:SC, 0:SC]).then_inc(w_turned, 1)
                pe.wait_ge(w_taken, 1)
                for kb in range(KB):
                    for h in range(H):
                        at = kb * SC + h * ES
                        last = nc.tensor.matmul(pr[:, 0, at:at + ES], wT[:, kb, h * P:(h + 1) * P],
                                                aT[:, h * ES:(h + 1) * ES], start=True, stop=True)
                last.then_inc(we_full, 1)
                pe.wait_ge(we_done, 1)

                def project(v):
                    pe.wait_ge(x_in, (v + 1) * 16)
                    for kb in range(KB):
                        last = nc.tensor.transpose(tr[:, 0, kb * P:(kb + 1) * P], xin[:, kb * P:(kb + 1) * P], ident[:])
                    last.then_inc(x_turned, 1)
                    pe.wait_ge(xT_done, v + 1)
                    for kb in range(KB):
                        flags = dict(start=(kb == 0), stop=(kb == KB - 1))
                        nc.tensor.matmul(pr[:, 0, 0:D], xT[:, kb], Wf[:, kb].rearrange("p h e -> p (h e)"), **flags)
                    for kb in range(KB):
                        flags = dict(start=(kb == 0), stop=(kb == KB - 1))
                        nc.tensor.matmul(pr[:, 1, 0:SC], xT[:, kb], Ws[:, kb], **flags)
                    for kb in range(KB):
                        flags = dict(start=(kb == 0), stop=(kb == KB - 1))
                        last = nc.tensor.matmul(ao[0:SC, 0:P], Ws[:, kb], xT[:, kb], **flags)
                    last.then_inc(h_full, 1)

                def unit(u, h, r):
                    pe.wait_ge(p_done, u + 1)
                    for t in range(TILES):
                        last = nc.tensor.transpose(tr[:, t // 4, t % 4 * P:(t % 4 + 1) * P], prob[:, t * P:(t + 1) * P], ident[:])
                    last.then_inc(pt_full, 1)
                    pe.wait_ge(pt_out, u + 1)
                    for t in range(TILES):
                        last = nc.tensor.matmul(ao[:, 0:HO], probT[:, t * P:(t + 1) * P], hx[:, t, h, :],
                                                start=(t == 0), stop=(t == TILES - 1))
                    last.then_inc(o_full, 1)

                with pe.Fori(0, NB) as b:
                    with pe.Fori(0, TILES) as t:
                        pe.wait_ge(h_taken, b * TILES + t + 1)
                        project(b * TILES + t)
                    units(pe, b, unit)
            pe.nop()

        @block.vector
        def _(dve):
            V = nc.vector
            with dve.If(dve.value_load(flag[0:1, 0:1]) != 0):
                for s in (h_taken, w_done, adj_taken):
                    dve.sem_inc(s, 1)
                dve.wait_ge(w_turned, 1)
                V.tensor_copy(aT[:], tr[0:HO, KB, 0:SC])
                V.tensor_copy(wT[:], tr[0:HO, 0:KB, :]).then_inc(w_taken, 1)
                dve.wait_ge(we_full, 1)
                V.tensor_copy(Ws[:], pr[:, 0, 0:KB * SC].rearrange("p (k s) -> p k s", k=KB)).then_inc(we_done, 1)

                def norm(s, t, width, eps, index, var_sem, rs_sem):
                    s.chain(dve, V.bn_stats(st[:], t[:]))
                    settled(dve)
                    s.chain(dve, V.bn_aggr(mv[:], st[:]))
                    V.tensor_scalar(vv[:], mv[:, 1:2], eps, None, ALU.add).then_inc(var_sem, 1)
                    dve.wait_ge(rs_sem, index + 1)
                    s.chain(dve, V.tensor_scalar(t[:], t[:], mv[:, 0:1], rs[:, 0:1], ALU.subtract, ALU.mult))

                def unit(s, u, h, r):
                    dve.wait_ge(adj_in, (u + 1) * 16)
                    V.tensor_copy(adjF[:], adjI[:]).then_inc(adj_taken, 1)
                    s.chain(dve, V.tensor_copy(es[:], sc[:, bass.ds(r, 1), h * ES:h * ES + TY].rearrange("p o t -> p (o t)")))
                    dve.wait_ge(adj_taken, u + 2)
                    for t in range(TY):
                        to = wt if t == 0 else part
                        s.chain(dve, V.tensor_scalar(part[:], dB[:, t, :], es[:, t:t + 1], None, ALU.add))
                        s.chain(dve, V.scalar_tensor_tensor(to[:], adjF[:], t + 1.0, part[:], ALU.is_equal, ALU.mult))
                        if t:
                            s.chain(dve, V.tensor_tensor(wt[:], wt[:], part[:], ALU.add))
                    s.chain(dve, V.scalar_tensor_tensor(wt[:], wt[:], SLOPE, wt[:], ALU.mult, ALU.max))
                    s.chain(dve, V.tensor_scalar(part[:], adjF[:], 0.0, NEG, ALU.is_equal, ALU.mult))
                    s.chain(dve, V.tensor_tensor(wt[:], wt[:], part[:], ALU.add))
                    V.tensor_reduce(nmax[:], wt[:], AX.X, ALU.max, negate=True).then_inc(w_done, 1)
                    dve.wait_ge(o_full, u + 1)
                    s.chain(dve, V.reciprocal(den[:], den[:]))
                    s.chain(dve, V.tensor_scalar(o[:], ao[:, 0:HO], den[:, 0:1], None, ALU.mult))
                    s.chain(dve, V.tensor_tensor(o[:], o[:], biasB[:, h * HO:(h + 1) * HO], ALU.add))
                    s.chain(dve, V.tensor_scalar(o[:], o[:], 0.0, None, ALU.max))
                    own = hx[:, bass.ds(r, 1), h, :].rearrange("p o e -> p (o e)")
                    s.chain(dve, V.tensor_tensor(o[:], o[:], own, ALU.add))
                    norm(s, o, HO, EPS_HEAD, u, var_done, rs_done)
                    s.chain(dve, V.tensor_tensor(o[:], o[:], gammaB[:, h * HO:(h + 1) * HO], ALU.mult))
                    dst = ho[:, bass.ds(r, 1), h * HO:(h + 1) * HO].rearrange("p o e -> p (o e)")
                    s.chain(dve, V.tensor_tensor(dst, o[:], betaB[:, h * HO:(h + 1) * HO], ALU.add))
                    assert s.n == UNIT_STEPS, s.n

                with dve.Fori(0, NB) as b:
                    dve.wait_ge(rows_free, b + 1)
                    settled(dve)
                    with dve.Fori(0, TILES) as t:
                        v = b * TILES + t
                        dve.wait_ge(x_turned, v + 2)
                        V.tensor_copy(xT[:], tr[:, 0, 0:D].rearrange("p (k i) -> p k i", k=KB)).then_inc(xT_done, 1)
                        dve.wait_ge(h_full, v + 1)
                        settled(dve)
                        V.tensor_copy(hx[:, bass.ds(t, 1)], pr[:, 0:1, 0:D].rearrange("p o (h e) -> p o h e", h=H))
                        V.tensor_copy(sc[:, bass.ds(t, 1)], pr[:, 1:2, 0:SC])
                        V.tensor_copy(rows[:, bass.ds(t * P, P)], ao[0:SC, 0:P]).then_inc(h_taken, 1)
                    dve.wait_ge(h_taken, (b + 1) * TILES + 1)
                    for h in range(H):
                        dve.wait_ge(ed_in, b * (16 * H) + 16 * (h + 1))
                        settled(dve)
                        with dve.Fori(0, TILES) as r:
                            s = Steps(unit_step)
                            u = b * (H * TILES) + (r + h * TILES)
                            s.rebase(u * UNIT_STEPS)
                            unit(s, u, h, r)
                    with dve.Fori(0, TILES) as r:
                        v = b * TILES + r
                        s = Steps(out_step)
                        s.rebase(v * OUT_STEPS)
                        dve.wait_ge(xr_in, (v + 1) * 16)
                        hr = ho[:, bass.ds(r, 1), :].rearrange("p o d -> p (o d)")
                        s.chain(dve, V.tensor_tensor(y[:], xin[:], hr, ALU.add))
                        norm(s, y, D, EPS_OUT, v, var2_done, rs2_done)
                        assert s.n == OUT_STEPS, s.n
                        dve.sem_inc(y_done, 1)
            dve.nop()


_INS = ["x", "adj", "L0_gnn_W", "L0_gnn_a_src", "L0_gnn_a_dst", "L0_gnn_bias", "L0_gnn_ln_gamma", "L0_gnn_ln_beta"]


def kernel(**inputs):
    import numpy as _np
    import concourse.bacc as _bacc
    from concourse import mybir as _mybir
    from concourse.bass_utils import run_bass_kernel_spmd as _run

    nc = _bacc.Bacc("TRN2", target_bir_lowering=False, num_devices=1, dynamic_dma_scratch_size=1024)
    arrays, args = {}, []
    for name in _INS:
        a = _np.ascontiguousarray(inputs[name])
        arrays[f"in_{name}_dram"] = a
        args.append(nc.dram_tensor(f"in_{name}_dram", a.shape, _mybir.dt.from_np(a.dtype), kind="ExternalInput").ap())
    out = nc.dram_tensor("out_0_dram", inputs["x"].shape, _mybir.dt.float32, kind="ExternalOutput").ap()
    adj_resnorm(nc, *args, out)
    r = _run(nc, [arrays], core_ids=[0])
    return r.results[0]["out_0_dram"]
```
